# Optimizing a Trainium2 kernel written in Bass

```python
import numpy as np
import jax
import jax.numpy as jnp

def _softmax(x, axis=-1):
    return jax.nn.softmax(x, axis=axis)

def _gelu(x):
    return jax.nn.gelu(x, approximate=True)

def _silu(x):
    return jax.nn.silu(x)

def _sigmoid(x):
    return jax.nn.sigmoid(x)

def _layernorm(x, axis=-1, eps=1e-05):
    m = jnp.mean(x, axis=axis, keepdims=True)
    v = jnp.var(x, axis=axis, keepdims=True)
    return (x - m) / jnp.sqrt(v + eps)

def _scatter_add(tgt, idx, src, axis=0):
    return tgt.at[idx].add(src)

def _segment_sum(src, seg, n):
    return jax.ops.segment_sum(src, seg, n)
kernel_name = 'mk_gnn_resnorm_d1_gnn_r8_96f6c5'

def setup_inputs(seed: int=0):
    np.random.seed(seed)
    _w = jnp.asarray

    def _rec_inputs():
        import jax
        import jax.numpy as jnp
        _gk = jax.random.key(seed)
        x = -0.000202 + 1 * jax.random.normal(jax.random.fold_in(_gk, 1), (6250, 128), jnp.float32)
        src = jax.random.randint(jax.random.fold_in(_gk, 2), (200000,), 0, 6250, jnp.int32)
        dst = jax.random.randint(jax.random.fold_in(_gk, 3), (200000,), 0, 6250, jnp.int32)
        _o = jnp.argsort(dst, stable=True)
        src = src[_o]
        dst = dst[_o]
        edge_attr_64 = 0.000189758 + 1.00013 * jax.random.normal(jax.random.fold_in(_gk, 11), (200000, 64), jnp.float32)
        return (x, src, dst, edge_attr_64)
    x, src, dst, edge_attr_64 = _rec_inputs()

    def _L0_gnn_setup():
        import jax, jax.numpy as jnp
        import numpy as np
        N_NODES = 6250
        N_EDGES = 100000
        IN_F = 128
        OUT_F = 128
        HEADS = 8
        HEAD_DIM = OUT_F // HEADS
        EDGE_F = 64
        key = jax.random.key(seed)
        ks = jax.random.split(key, 12)
        s = 0.05
        return {'node_features': jax.random.normal(ks[0], (N_NODES, IN_F), jnp.float32), 'edge_index': jax.random.randint(ks[1], (2, N_EDGES), 0, N_NODES, jnp.int32), 'edge_features': jax.random.normal(ks[2], (N_EDGES, EDGE_F), jnp.float32), 'Wq': jax.random.normal(ks[3], (IN_F, OUT_F), jnp.float32) * s, 'bq': jnp.zeros((OUT_F,), jnp.float32), 'Wk': jax.random.normal(ks[4], (IN_F, OUT_F), jnp.float32) * s, 'bk': jnp.zeros((OUT_F,), jnp.float32), 'Wv': jax.random.normal(ks[5], (IN_F, OUT_F), jnp.float32) * s, 'bv': jnp.zeros((OUT_F,), jnp.float32), 'We': jax.random.normal(ks[6], (EDGE_F, HEADS), jnp.float32) * s, 'be': jnp.zeros((HEADS,), jnp.float32), 'Wo': jax.random.normal(ks[7], (OUT_F, OUT_F), jnp.float32) * s, 'bo': jnp.zeros((OUT_F,), jnp.float32)}
    _L0_gnn_all = _L0_gnn_setup()
    _L0_gnn_in = {k: v for k, v in _L0_gnn_all.items() if k in ('Wq', 'bq', 'Wk', 'bk', 'Wv', 'bv', 'We', 'be', 'Wo', 'bo')}
    del _L0_gnn_all
    return {'x': x, 'src': src, 'dst': dst, 'edge_attr_64': edge_attr_64, 'L0_gnn_Wq': _L0_gnn_in['Wq'], 'L0_gnn_bq': _L0_gnn_in['bq'], 'L0_gnn_Wk': _L0_gnn_in['Wk'], 'L0_gnn_bk': _L0_gnn_in['bk'], 'L0_gnn_Wv': _L0_gnn_in['Wv'], 'L0_gnn_bv': _L0_gnn_in['bv'], 'L0_gnn_We': _L0_gnn_in['We'], 'L0_gnn_be': _L0_gnn_in['be'], 'L0_gnn_Wo': _L0_gnn_in['Wo'], 'L0_gnn_bo': _L0_gnn_in['bo']}

def reference(x, src, dst, edge_attr_64, L0_gnn_Wq, L0_gnn_bq, L0_gnn_Wk, L0_gnn_bk, L0_gnn_Wv, L0_gnn_bv, L0_gnn_We, L0_gnn_be, L0_gnn_Wo, L0_gnn_bo):
    import jax
    import jax.numpy as jnp

    def _L0_gnn_ref(node_features, edge_index, edge_features, Wq, bq, Wk, bk, Wv, bv, We, be, Wo, bo):
        import jax, jax.numpy as jnp
        import numpy as np
        N_NODES = 6250
        N_EDGES = 100000
        IN_F = 128
        OUT_F = 128
        HEADS = 8
        HEAD_DIM = OUT_F // HEADS
        EDGE_F = 64
        n_nodes = node_features.shape[0]
        scale = HEAD_DIM ** (-0.5)
        sources = edge_index[0]
        targets = edge_index[1]
        q = (node_features @ Wq + bq).reshape(n_nodes, HEADS, HEAD_DIM)
        k = (node_features @ Wk + bk).reshape(n_nodes, HEADS, HEAD_DIM)
        v = (node_features @ Wv + bv).reshape(n_nodes, HEADS, HEAD_DIM)
        q_t = q[targets]
        k_s = k[sources]
        v_s = v[sources]
        scores = jnp.sum(q_t * k_s, axis=-1) * scale + (edge_features @ We + be)
        max_s = jax.ops.segment_max(scores, targets, num_segments=n_nodes)
        e = jnp.exp(scores - max_s[targets])
        denom = jax.ops.segment_sum(e, targets, num_segments=n_nodes) + 1e-10
        probs = e / denom[targets]
        weighted = (probs[:, :, None] * v_s).reshape(scores.shape[0], -1)
        agg = jax.ops.segment_sum(weighted, targets, num_segments=n_nodes)
        return agg @ Wo + bo
    edge_index = jnp.stack([src, dst])
    x = _layernorm(x + _L0_gnn_ref(x, edge_index, edge_attr_64, L0_gnn_Wq, L0_gnn_bq, L0_gnn_Wk, L0_gnn_bk, L0_gnn_Wv, L0_gnn_bv, L0_gnn_We, L0_gnn_be, L0_gnn_Wo, L0_gnn_bo), axis=-1)
    return x

_drawn_inputs = setup_inputs


def setup_inputs(seed=0):
    import zlib

    import numpy as np

    out = dict(_drawn_inputs(seed))
    spreads = {'L0_gnn_bq': (0.0, 2.0),
     'L0_gnn_bk': (0.0, 2.0),
     'L0_gnn_bv': (0.0, 0.1),
     'L0_gnn_be': (0.0, 2.0),
     'L0_gnn_bo': (0.0, 0.1)}
    factors = {}
    for name, (base, spread) in spreads.items():
        noise = np.random.default_rng([zlib.crc32(name.encode()), seed]).standard_normal(out[name].shape)
        drawn = base * np.exp(spread * noise) if base else spread * noise
        out[name] = jnp.asarray(drawn.astype(out[name].dtype))
    for name, factor in factors.items():
        out[name] = (out[name] * factor).astype(out[name].dtype)
    return out
```

```python
from contextlib import ExitStack

import concourse.bass as bass
from concourse import mybir

P = 128
F32 = mybir.dt.float32
I32 = mybir.dt.int32
ALU = mybir.AluOpType
ACT = mybir.ActivationFunctionType
AX = mybir.AxisListType

QUAD = 4
FAR = -3.0e38
LN_EPS = 1e-5
DEN_EPS = 1e-10


class Line:

    def __init__(self, marks, semaphore):
        self.marks, self.semaphore, self.count, self.items = marks, semaphore, 0, []

    def do(self, emit, mark=None):
        if mark is not None:
            mark = mark if isinstance(mark, tuple) else (mark,)
            self.count += 1
            assert mark not in self.marks, mark
            self.marks[mark] = (self.semaphore, self.count)
        self.items.append(("do", emit, mark))

    def wait(self, *mark):
        self.items.append(("wait", mark, None))

    def wait_dma(self, semaphore, value):
        self.items.append(("dma", semaphore, value))

    def emit(self, engine):
        for kind, a, b in self.items:
            if kind == "dma":
                engine.wait_ge(a, b)
            elif kind == "wait":
                engine.wait_ge(*self.marks[a])
            else:
                instruction = a()
                if b is not None:
                    instruction.then_inc(self.semaphore, 1)


def graph_attention(nc, x, x_t, src, dst, edge_t, Wq, bq, Wk, bk, Wv, bv, We, be, Wo, bo, out):
    N, D = x.shape
    E = src.shape[0]
    EF, H = We.shape
    HD = D // H
    NB = -(-N // P)
    SLACK = 4 * int((P * E / N) ** 0.5)
    L = -(-(P * E // N + SLACK) // P)
    C = P * L
    G = -(-L // QUAD)
    STEP = [(g * QUAD, min(L, g * QUAD + QUAD)) for g in range(G)]
    SCALE = float(HD) ** -0.5
    RP = max(r for r in range(1, P) if E % r == 0)
    RC = E // RP
    NS = NB + 1
    LAST = N - (NB - 1) * P
    KV, QKV = 2 * D, 3 * D
    WV = D + H
    STAGES = 8
    AHEAD = 2

    ctx = ExitStack()
    with ctx:
        def sb(name, shape, dt=F32):
            return ctx.enter_context(nc.sbuf_tensor(name, shape, dt))

        def ps(name, shape):
            return ctx.enter_context(nc.psum_tensor(name, shape, F32))

        def sem(name):
            return ctx.enter_context(nc.semaphore(name))

        kv_table = nc.dram_tensor("kv_table", [N, KV], F32).ap()
        starts_dram = nc.dram_tensor("starts_dram", [NS, 1], I32).ap()

        ident = sb("ident", [P, P])
        iota_i = sb("iota_i", [P, P], I32)
        iota_n = sb("iota_n", [P, P])
        ones = sb("ones", [P, P])
        w_qkv = sb("w_qkv", [P, QKV])
        w_o = sb("w_o", [P, D])
        w_e = sb("w_e", [EF + 1, H])
        bias_row = sb("bias_row", [1, QKV + D])
        bias_bc = sb("bias_bc", [P, QKV + D])
        q_all = sb("q_all", [P, NB, D])
        kv_buf = sb("kv_buf", [P, 2, L, KV])
        onehot = sb("onehot", [P, 2, L, P])
        onehot_t = sb("onehot_t", [P, 2, QUAD * P])
        edge_f = [sb(f"edge_f{i}", [EF + 1, C]) for i in range(2)]
        src_i = sb("src_i", [P, 2, L], I32)
        dst_i = sb("dst_i", [P, 2, L], I32)
        dst_f = sb("dst_f", [P, 2, L])
        dst_rel = sb("dst_rel", [P, 2, L])
        prod = sb("prod", [P, 2, QUAD * D])
        score = sb("score", [P, 2, H, L])
        run_fwd = sb("run_fwd", [P, H * L])
        run_max = sb("run_max", [P, H, L])
        end_fwd = sb("end_fwd", [P, H, L])
        end_bwd = sb("end_bwd", [P, H, L])
        not_first = sb("not_first", [P, L])
        not_last = sb("not_last", [P, L])
        run_far = sb("run_far", [P, L])
        cand = sb("cand", [P, 2, H, L])
        shifted = sb("shifted", [P, H, L])
        ends = sb("ends", [P, 4, H])
        seq_val = sb("seq_val", [H, 2 * P])
        seq_dst = sb("seq_dst", [H, 2 * P])
        seq_ef = sb("seq_ef", [H, 2 * P])
        seq_eb = sb("seq_eb", [H, 2 * P])
        seq_ne = sb("seq_ne", [H, 2 * P])
        seq_f = sb("seq_f", [H, 2 * P])
        seq_b = sb("seq_b", [H, 2 * P])
        weight = sb("weight", [P, 2, H, L])
        wv = sb("wv", [P, 2, QUAD, WV])
        den = sb("den", [P, H])
        rec = sb("rec", [P, H])
        agg_n = sb("agg_n", [P, D])
        y_sum = sb("y_sum", [P, D])
        agg_t = sb("agg_t", [P, D])
        x_blk = sb("x_blk", [P, 2, D])
        stats = sb("stats", [P, 6])
        moments = sb("moments", [P, 2])
        rstd = sb("rstd", [P, 2])
        eps_c = sb("eps_c", [P, 1])
        y_out = sb("y_out", [P, 2, D])
        xt = onehot[:, :, :, :].rearrange("p a l n -> p (a l n)")[:, 0:N]
        kv_stage = kv_buf[:, 0, 0:STAGES, :]
        dst2d_i = kv_buf[0:RP, 0, STAGES:STAGES + -(-RC // KV), :].rearrange("p a b -> p (a b)")[:, 0:RC].bitcast(I32)
        row_i = kv_buf[0:NS, 0, 16:16 + -(-RC // KV), :].rearrange("p a b -> p (a b)")[:, 0:RC].bitcast(I32)
        row_f = kv_buf[0:NS, 0, 24:24 + -(-RC // KV), :].rearrange("p a b -> p (a b)")[:, 0:RC]
        assert 24 + -(-RC // KV) <= L and STAGES * KV >= RC and 2 * L * P >= N
        border_i = sb("border_i", [P, NS], I32)
        border = sb("border", [P, NS])
        border_p = sb("border_p", [P, 1])
        border_pi = sb("border_pi", [P, 1], I32)
        last_f = sb("last_f", [P, 1])
        below = sb("below", [P, NS])
        rows_f = sb("rows_f", [P, 1])
        rows_i = sb("rows_i", [P, 1], I32)
        cnt = sb("cnt", [P, 1])
        start_f = sb("start_f", [P, 2])
        start_i = sb("start_i", [P, 1], I32)
        start_row = sb("start_row", [1, NS], I32)

        ps_t = [ps(f"ps_t{i}", [P, 512]) for i in range(2)]
        ps_q = [ps(f"ps_q{i}", [P, 512]) for i in range(2)]
        ps_e = ps("ps_e", [P, 512])
        ps_a = [ps(f"ps_a{i}", [P, 512]) for i in range(2)]
        ps_s = ps("ps_s", [P, 512])

        back_max = ps_e[:, L * H:L * H + 2 * H]
        assert L * H + 2 * H <= 512

        def sums(b):
            return ps_a[b % 2][:, 0:WV]

        def turned(b):
            return ps_a[b % 2][:, WV:WV + D]

        def projected(b):
            return ps_a[b % 2][:, WV + D:WV + 2 * D]

        s_w = sem("s_w")
        s_xt = sem("s_xt")
        s_dst2d = sem("s_dst2d")
        s_rows = sem("s_rows")
        s_start = sem("s_start")
        s_row = sem("s_row")
        s_table = [sem(f"s_table{i}") for i in range(STAGES)]
        s_src = [sem(f"s_src{i}") for i in range(2)]
        s_dst = [sem(f"s_dst{i}") for i in range(2)]
        s_edge = [sem(f"s_edge{i}") for i in range(2)]
        s_x = [sem(f"s_x{i}") for i in range(2)]
        s_kv = [[sem(f"s_kv{i}_{g}") for g in range(G)] for i in range(2)]
        s_y = [sem(f"s_y{i}") for i in range(2)]
        marks = {}
        pool, act, dve, pe = (Line(marks, sem(f"s_{n}")) for n in ("pool", "act", "dve", "pe"))
        sp = Line(marks, None)
        V, T, S = nc.vector, nc.tensor, nc.scalar

        def kv_ready(b, g):
            return s_kv[b % 2][g], 16 * (STEP[g][1] - STEP[g][0]) * (b // 2 + 1)

        def rows(b):
            return P if b < NB - 1 else LAST

        pool.do(lambda: nc.gpsimd.memset(ident[:, :], 0.0), "ident zero")
        pool.do(lambda: nc.gpsimd.iota(iota_i[:, :], [[1, P]], base=0, channel_multiplier=0))
        pool.do(lambda: nc.gpsimd.iota(border_i[:, :], [[P, NS]], base=0, channel_multiplier=0))
        pool.do(lambda: nc.gpsimd.iota(border_pi[:, :], [[0, 1]], base=0, channel_multiplier=P), "iotas")
        pool.wait("ident zero")
        pool.do(lambda: nc.gpsimd.affine_select(
            out=ident[:, :], in_=ident[:, :], compare_op=ALU.not_equal, fill=1.0, base=0,
            pattern=[[-1, P]], channel_multiplier=1), "ident")

        dve.do(lambda: V.memset(ones[:, :], 1.0), "ones")
        dve.do(lambda: V.memset(eps_c[:, :], LN_EPS))
        dve.do(lambda: V.memset(x_blk[:, :, :], 0.0), "x zero")
        for e in edge_f:
            dve.do(lambda e=e: V.memset(e[EF:EF + 1, :], 1.0), ("edge ones", e is edge_f[1]))
        dve.wait("iotas")
        dve.do(lambda: V.tensor_copy(iota_n[:, :], iota_i[:, :]), "iota_n")
        dve.do(lambda: V.tensor_copy(border[:, :], border_i[:, :]))
        dve.do(lambda: V.tensor_copy(border_p[:, :], border_pi[:, :]))

        dve.wait_dma(s_dst2d, 16)
        dve.do(lambda: V.tensor_copy(last_f[0:RP, :], dst2d_i[:, RC - 1:RC]), "row last")
        dve.wait("row last")
        dve.do(lambda: V.tensor_scalar(below[0:RP, :], border[0:RP, :], last_f[0:RP, 0:1], None,
                                       ALU.is_gt), "rows below")
        pe.wait("rows below")
        pe.do(lambda: T.matmul(ps_s[0:NS, 0:1], below[0:RP, :], ones[0:RP, 0:1],
                               start=True, stop=True), "rows counted")
        dve.wait("rows counted")
        dve.do(lambda: V.tensor_scalar(rows_f[0:NS, :], ps_s[0:NS, 0:1], float(RP - 1), None,
                                       ALU.min), "border row")
        dve.wait("border row")
        dve.do(lambda: V.tensor_copy(rows_i[0:NS, :], rows_f[0:NS, :]), "border row int")
        pool.wait("border row int")
        pool.do(lambda: nc.gpsimd.indirect_dma_start(
            row_i, None, dst.rearrange("(r c) -> r c", c=RC),
            bass.IndirectOffsetOnAxis(ap=rows_i[0:NS, 0:1], axis=0)).then_inc(s_rows, 16))

        pe.wait_dma(s_w, 16 * 10)
        pe.wait("border row")
        pe.do(lambda: T.matmul(ps_s[:, 0:QKV + D], ones[0:1, :], bias_row[:, :],
                               start=True, stop=True), "bias spread")
        dve.wait("bias spread")
        dve.do(lambda: V.tensor_copy(bias_bc[:, :], ps_s[:, 0:QKV + D]), "bias")

        dve.do(lambda: V.memset(q_all[:, NB - 1, :], 0.0), "q zero")
        pe.wait_dma(s_xt, 16)
        dve.wait("bias")
        dve.wait("q zero")

        def project_nodes(b):
            n = rows(b)
            bank = ps_q[b % 2]
            if b >= 2:
                pe.wait("staged", b - 2)
            pe.do(lambda: T.matmul(bank[0:n, 0:QKV], xt[:, b * P:b * P + n], w_qkv[:, :],
                                   start=True, stop=True), ("projected nodes", b))
            dve.wait("projected nodes", b)
            dve.do(lambda: V.tensor_tensor(q_all[0:n, b, :], bank[0:n, 0:D], bias_bc[0:n, 0:D], ALU.add))
            if b >= STAGES:
                dve.wait_dma(s_table[b % STAGES], 16 * (b // STAGES))
            dve.do(lambda: V.tensor_tensor(kv_stage[0:n, b % STAGES, :], bank[0:n, D:QKV],
                                           bias_bc[0:n, D:QKV], ALU.add), ("staged", b))

        def find_windows():
            dve.wait_dma(s_rows, 16)
            dve.do(lambda: V.tensor_copy(row_f, row_i), "row")
            dve.wait("row")
            dve.do(lambda: V.tensor_scalar(row_f, row_f, border_p[0:NS, 0:1], None, ALU.is_lt), "row below")
            dve.wait("row below")
            dve.do(lambda: V.tensor_reduce(cnt[0:NS, :], row_f, AX.X, ALU.add), "row count")
            dve.wait("row count")
            dve.do(lambda: V.scalar_tensor_tensor(
                out=start_f[0:NS, 0:1], in0=rows_f[0:NS, :], scalar=float(RC), in1=cnt[0:NS, :],
                op0=ALU.mult, op1=ALU.add), "border edge")
            dve.wait("border edge")
            dve.do(lambda: V.tensor_scalar(start_f[0:NS, 1:2], start_f[0:NS, 0:1], float(E - C), None,
                                           ALU.min), "start")
            dve.wait("start")
            dve.do(lambda: V.tensor_copy(start_i[0:NS, :], start_f[0:NS, 1:2]), "start int")

        for b in range(NB):
            project_nodes(b)
            if b == 4:
                find_windows()
        dve.wait("staged", NB - 1)
        dve.do(lambda: V.tensor_scalar(q_all[:, :, :], q_all[:, :, :], SCALE, None, ALU.mult), "q scaled")
        dve.wait("q scaled")

        pool.wait("start int")
        pool.do(lambda: nc.gpsimd.dma_start(starts_dram, start_i[0:NS, :]).then_inc(s_start, 16))
        pool.wait_dma(s_start, 16)
        pool.do(lambda: nc.gpsimd.dma_start(start_row[:, :], starts_dram.rearrange("s a -> a s"))
                .then_inc(s_row, 16))
        pool.wait_dma(s_row, 16)
        for i in range(STAGES):
            pool.wait_dma(s_table[i], 16 * len(range(i, NB, STAGES)))

        for b in range(NB):
            pool.wait_dma(s_src[b % 2], 16 * (b // 2 + 1))
            for g, (t0, t1) in enumerate(STEP):
                if b >= 2:
                    pool.wait("weighted", (b - 2) * G + g)
                for t in range(t0, t1):
                    pool.do(lambda b=b, t=t, g=g: nc.gpsimd.indirect_dma_start(
                        kv_buf[:, b % 2, t, :], None, kv_table,
                        bass.IndirectOffsetOnAxis(ap=src_i[:, b % 2, t:t + 1], axis=0))
                        .then_inc(s_kv[b % 2][g], 16))

        def indices(b):
            i = b % 2
            dve.wait_dma(s_dst[i], 16 * (b // 2 + 1))
            dve.do(lambda: V.tensor_copy(dst_f[:, i, :], dst_i[:, i, :]), ("dst", b))
            dve.wait("dst", b)
            dve.do(lambda: V.tensor_scalar(dst_rel[:, i, :], dst_f[:, i, :], float(-P * b), None,
                                           ALU.add), ("dst rel", b))
            dve.wait("dst rel", b)

        def build_onehot(q):
            b, g = divmod(q, G)
            if g == 0:
                indices(b)
            if b >= 2:
                dve.wait("summed", q - 2 * G)
            for t in range(*STEP[g]):
                dve.do(lambda t=t: V.tensor_scalar(
                    onehot[:, b % 2, t, :], iota_n[:, :], dst_rel[:, b % 2, t:t + 1], None,
                    ALU.is_equal), ("onehot", q) if t == STEP[g][1] - 1 else None)

        def multiply(q):
            b, (t0, t1) = q // G, STEP[q % G]
            n = t1 - t0
            dve.wait("q by edge", q)
            dve.wait_dma(*kv_ready(b, q % G))
            if q >= 2:
                dve.wait("dot", q - 2)
            dve.do(lambda: V.tensor_tensor(
                prod[:, q % 2, 0:n * D].rearrange("p (t d) -> p t d", d=D),
                ps_q[q % 2][:, 0:n * D].rearrange("p (t d) -> p t d", d=D),
                kv_buf[:, b % 2, t0:t1, 0:D], ALU.mult), ("product", q))

        def dot(q):
            b, (t0, t1) = q // G, STEP[q % G]
            dve.wait("product", q)
            dve.do(lambda: V.tensor_reduce(
                score[:, b % 2, :, t0:t1].rearrange("p h t -> p t h"),
                prod[:, q % 2, 0:(t1 - t0) * D].rearrange("p (t h d) -> p t h d", h=H, d=HD),
                AX.X, ALU.add), ("dot", q))

        def weigh(q):
            b, (t0, t1) = q // G, STEP[q % G]
            dve.wait("weights", b)
            if q >= 2:
                dve.wait("summed", q - 2)
            dve.do(lambda: V.tensor_tensor(
                wv[:, q % 2, 0:t1 - t0, 0:D].rearrange("p t (h d) -> p t h d", d=HD),
                kv_buf[:, b % 2, t0:t1, D:KV].rearrange("p t (h d) -> p t h d", d=HD),
                weight[:, b % 2, :, t0:t1].rearrange("p h (t a) -> p t h a", a=1)
                .to_broadcast([P, t1 - t0, H, HD]), ALU.mult), ("weighted", q))

        def maxima(b):
            i = b % 2
            d = dst_f[:, i, :]
            s = score[:, i, :, :]

            def flat(a):
                return a.rearrange("p h t -> p (h t)")

            def per_edge(a, n):
                return a.rearrange("p (a t) -> p a t", a=1).to_broadcast([P, H, n])

            def by_end(a):
                return a.rearrange("h (p e) -> h e p", e=2)

            dve.wait("edge terms", b)
            dve.wait("dot", (b + 1) * G - 1)
            dve.do(lambda: V.tensor_tensor(s, s, ps_e[:, 0:L * H].rearrange("p (t h) -> p h t", h=H),
                                           ALU.add), ("score", b))
            dve.do(lambda: V.memset(end_fwd[:, :, 0:1], FAR))
            dve.do(lambda: V.memset(end_bwd[:, :, L - 1:L], FAR))
            dve.do(lambda: V.tensor_tensor(run_far[:, 1:L], d[:, 1:L], d[:, 0:L - 1], ALU.not_equal),
                   ("changes", b))
            dve.wait("changes", b)
            dve.do(lambda: V.tensor_scalar(end_fwd[:, :, 1:L], per_edge(run_far[:, 1:L], L - 1), FAR,
                                           None, ALU.mult))
            dve.do(lambda: V.tensor_scalar(end_bwd[:, :, 0:L - 1], per_edge(run_far[:, 1:L], L - 1),
                                           FAR, None, ALU.mult), ("run ends", b))
            dve.wait("run ends", b)
            dve.do(lambda: V.tensor_tensor_scan(run_fwd[:, :], flat(end_fwd[:, :, :]), flat(s), FAR,
                                                ALU.add, ALU.max), ("forward", b))
            dve.wait("forward", b)
            dve.do(lambda: V.tensor_tensor_scan(
                flat(run_max[:, :, :])[:, ::-1], flat(end_bwd[:, :, :])[:, ::-1], run_fwd[:, ::-1],
                FAR, ALU.add, ALU.max), ("backward", b))
            dve.wait("backward", b)
            dve.do(lambda: V.tensor_copy(ends[:, 0, :], run_max[:, :, 0]))
            dve.do(lambda: V.tensor_copy(ends[:, 1, :], run_max[:, :, L - 1]))
            dve.do(lambda: V.tensor_copy(ends[:, 2, :], d[:, 0:1].to_broadcast([P, H])))
            dve.do(lambda: V.tensor_copy(ends[:, 3, :], d[:, L - 1:L].to_broadcast([P, H])), ("ends", b))
            pe.wait("ends", b)
            for k in range(4):
                pe.do(lambda k=k: T.transpose(ps_s[0:H, k * P:(k + 1) * P], ends[:, k, :], ident[:, :]),
                      ("ends turned", b) if k == 3 else None)
            dve.do(lambda: V.tensor_scalar(not_first[:, :], d, d[:, 0:1], FAR, ALU.not_equal, ALU.mult))
            dve.do(lambda: V.tensor_scalar(not_last[:, :], d, d[:, L - 1:L], FAR, ALU.not_equal,
                                           ALU.mult))
            dve.wait("ends turned", b)
            dve.do(lambda: V.tensor_copy(by_end(seq_val[:, :]),
                                         ps_s[0:H, 0:2 * P].rearrange("h (e p) -> h e p", e=2)))
            dve.do(lambda: V.tensor_copy(by_end(seq_dst[:, :]),
                                         ps_s[0:H, 2 * P:4 * P].rearrange("h (e p) -> h e p", e=2)),
                   ("sequence", b))
            dve.wait("sequence", b)
            dve.do(lambda: V.memset(seq_ef[:, 0:1], FAR))
            dve.do(lambda: V.memset(seq_eb[:, 2 * P - 1:2 * P], FAR))
            dve.do(lambda: V.tensor_tensor(seq_ne[:, 1:2 * P], seq_dst[:, 1:2 * P],
                                           seq_dst[:, 0:2 * P - 1], ALU.not_equal), ("seq changes", b))
            dve.wait("seq changes", b)
            dve.do(lambda: V.tensor_scalar(seq_ef[:, 1:2 * P], seq_ne[:, 1:2 * P], FAR, None, ALU.mult))
            dve.do(lambda: V.tensor_scalar(seq_eb[:, 0:2 * P - 1], seq_ne[:, 1:2 * P], FAR, None,
                                           ALU.mult), ("seq ends", b))
            dve.wait("seq ends", b)
            dve.do(lambda: V.tensor_tensor_scan(seq_f[:, :], seq_ef[:, :], seq_val[:, :], FAR, ALU.add,
                                                ALU.max), ("seq forward", b))
            dve.wait("seq forward", b)
            dve.do(lambda: V.tensor_tensor_scan(seq_b[:, ::-1], seq_eb[:, ::-1], seq_f[:, ::-1], FAR,
                                                ALU.add, ALU.max), ("seq backward", b))
            pe.wait("seq backward", b)
            for k in range(2):
                pe.do(lambda k=k: T.transpose(
                    back_max[:, k * H:(k + 1) * H], seq_b[:, :].rearrange("h (p e) -> h p e", e=2)[:, :, k],
                    ident[0:H, 0:H]), ("crossing", b) if k == 1 else None)
            dve.wait("crossing", b)
            for k, away in enumerate((not_first, not_last)):
                dve.do(lambda k=k, away=away: V.tensor_tensor(
                    cand[:, k, :, :],
                    back_max[:, k * H:(k + 1) * H].rearrange("p (h a) -> p h a", a=1).to_broadcast([P, H, L]),
                    per_edge(away[:, :], L), ALU.add), ("candidates", b) if k == 1 else None)
            dve.wait("candidates", b)
            dve.do(lambda: V.tensor_tensor(cand[:, 0, :, :], cand[:, 0, :, :], cand[:, 1, :, :], ALU.max),
                   ("larger", b))
            dve.wait("larger", b)
            dve.do(lambda: V.tensor_tensor(run_max[:, :, :], run_max[:, :, :], cand[:, 0, :, :], ALU.max),
                   ("maximum", b))
            dve.wait("maximum", b)
            if b >= 1:
                dve.wait("weights", b - 1)
            dve.do(lambda: V.tensor_tensor(shifted[:, :, :], s, run_max[:, :, :], ALU.subtract),
                   ("shifted", b))

        def divide(b):
            dve.wait("summed", (b + 1) * G - 1)
            dve.do(lambda: V.tensor_scalar(den[:, :], sums(b)[:, D:WV], DEN_EPS, None, ALU.add), ("den", b))
            dve.wait("den", b)
            dve.do(lambda: V.reciprocal(rec[:, :], den[:, :]), ("rec", b))
            dve.wait("rec", b)
            if b >= 1:
                dve.wait("aggregate turned", b - 1)
            dve.do(lambda: V.tensor_tensor(
                agg_n[:, :].rearrange("p (h d) -> p h d", d=HD),
                sums(b)[:, 0:D].rearrange("p (h d) -> p h d", d=HD),
                rec[:, :].rearrange("p (h a) -> p h a", a=1).to_broadcast([P, H, HD]), ALU.mult),
                ("aggregate", b))

        def residual(b):
            dve.wait("times Wo", b)
            dve.wait_dma(s_x[b % 2], 16 * (b // 2 + 1))
            dve.do(lambda: V.tensor_tensor(y_sum[:, :], projected(b), x_blk[:, b % 2, :], ALU.add),
                   ("residual", b))
            dve.wait("residual", b)
            dve.do(lambda: V.tensor_tensor(y_sum[:, :], y_sum[:, :], bias_bc[:, QKV:QKV + D], ALU.add),
                   ("y", b))
            dve.wait("y", b)
            dve.do(lambda: V.bn_stats(stats[:, :], y_sum[:, :]), ("stats", b))
            dve.wait("stats", b)
            dve.do(lambda: V.bn_aggr(moments[:, :], stats[:, :]), ("moments", b))

        def normalise(b):
            dve.wait("rstd", b)
            if b >= 2:
                dve.wait_dma(s_y[b % 2], 16 * (b // 2))
            dve.do(lambda: V.tensor_scalar(y_out[:, b % 2, :], y_sum[:, :], moments[:, 0:1], rstd[:, 1:2],
                                           ALU.subtract, ALU.mult), ("normal", b))

        def turn_onehot(q):
            b, (t0, t1) = q // G, STEP[q % G]
            pe.wait("onehot", q)
            if q >= 2:
                pe.wait("onehot copied", q - 2)
            for t in range(t0, t1):
                pe.do(lambda t=t: T.transpose(ps_t[q % 2][:, (t - t0) * P:(t - t0 + 1) * P],
                                              onehot[:, b % 2, t, :], ident[:, :]),
                      ("onehot turned", q) if t == t1 - 1 else None)

        def spread_q(q):
            b, (t0, t1) = q // G, STEP[q % G]
            pe.wait("onehot copied", q)
            if q >= 2:
                pe.wait("product", q - 2)
            for t in range(t0, t1):
                pe.do(lambda t=t: T.matmul(
                    ps_q[q % 2][:, (t - t0) * D:(t - t0 + 1) * D],
                    onehot_t[:, q % 2, (t - t0) * P:(t - t0 + 1) * P], q_all[:, b, :],
                    start=True, stop=True), ("q by edge", q) if t == t1 - 1 else None)
            if t0 == 0:
                pe.wait_dma(s_edge[b % 2], 16 * (b // 2 + 1))
                if b >= 1:
                    pe.wait("candidates", b - 1)
            for t in range(t0, t1):
                pe.do(lambda t=t: T.matmul(ps_e[:, t * H:(t + 1) * H], edge_f[b % 2][:, t:C:L], w_e[:, :],
                                           start=True, stop=True),
                      ("edge terms", b) if t == L - 1 else None)

        def sum_step(q):
            b, (t0, t1) = q // G, STEP[q % G]
            pe.wait("weighted", q)
            pe.wait("weights beside", q)
            if t0 == 0 and b >= 2:
                pe.wait("residual", b - 2)
            for t in range(t0, t1):
                pe.do(lambda t=t: T.matmul(sums(b), onehot[:, b % 2, t, :], wv[:, q % 2, t - t0, :],
                                           start=(t == 0), stop=(t == L - 1)),
                      ("summed", q) if t == t1 - 1 else None)

        def turn_aggregate(b):
            pe.wait("aggregate", b)
            pe.do(lambda: T.transpose(turned(b), agg_n[:, :], ident[:, :]), ("aggregate turned", b))

        def times_wo(b):
            pe.wait("turned copied", b)
            pe.do(lambda: T.matmul(projected(b), agg_t[:, :], w_o[:, :], start=True, stop=True),
                  ("times Wo", b))

        def copy_onehot(q):
            n = (STEP[q % G][1] - STEP[q % G][0]) * P
            act.wait("onehot turned", q)
            if q >= 2:
                act.wait("q by edge", q - 2)
            act.do(lambda: S.copy(onehot_t[:, q % 2, 0:n], ps_t[q % 2][:, 0:n]), ("onehot copied", q))

        def exponentials(b):
            act.wait("shifted", b)
            act.do(lambda: S.activation(weight[:, b % 2, :, :], shifted[:, :, :], ACT.Exp), ("weights", b))

        def copy_weights(q):
            b, (t0, t1) = q // G, STEP[q % G]
            act.wait("weights", b)
            if q >= 2:
                act.wait("summed", q - 2)
            act.do(lambda: S.copy(wv[:, q % 2, 0:t1 - t0, D:WV],
                                  weight[:, b % 2, :, t0:t1].rearrange("p h t -> p t h")),
                   ("weights beside", q))

        def copy_turned(b):
            act.wait("aggregate turned", b)
            if b >= 1:
                act.wait("times Wo", b - 1)
            act.do(lambda: S.copy(agg_t[:, :], turned(b)), ("turned copied", b))

        def inverse_deviation(b):
            act.wait("moments", b)
            act.do(lambda: S.activation(rstd[:, 0:1], moments[:, 1:2], ACT.Ln, bias=eps_c[:, 0:1]),
                   ("log", b))
            act.wait("log", b)
            act.do(lambda: S.activation(rstd[:, 1:2], rstd[:, 0:1], ACT.Exp, scale=-0.5), ("rstd", b))

        pe.wait("ident")
        pe.wait("q scaled")
        pe.wait_dma(s_w, 16 * 10)
        pe.wait("edge ones", True)
        act.wait("x zero")
        for q in range(AHEAD):
            build_onehot(q)
        for q in range((NB + 2) * G):
            b, g = divmod(q, G)
            if q < NB * G:
                turn_onehot(q)
                copy_onehot(q)
            if 1 <= q <= NB * G:
                spread_q(q - 1)
            if g == 0 and 1 <= b <= NB:
                maxima(b - 1)
            if q + AHEAD < NB * G:
                build_onehot(q + AHEAD)
            if q < NB * G:
                multiply(q)
            if g == 0 and 1 <= b <= NB:
                exponentials(b - 1)
            if 1 <= b <= NB:
                copy_weights(q - G)
                weigh(q - G)
            if q < NB * G:
                dot(q)
            if G < q <= (NB + 1) * G:
                sum_step(q - 1 - G)
            if 2 <= b:
                if g == 1:
                    divide(b - 2)
                if g == 2:
                    turn_aggregate(b - 2)
                    copy_turned(b - 2)
                if g == 3:
                    times_wo(b - 2)
                if g == 4:
                    residual(b - 2)
                if g == 5:
                    inverse_deviation(b - 2)
                if g == 7:
                    normalise(b - 2)

        sp.do(lambda: nc.sync.dma_start(dst2d_i, dst.rearrange("(r c) -> r c", c=RC)).then_inc(s_dst2d, 16))
        for i, w in enumerate((Wq, Wk, Wv)):
            sp.do(lambda i=i, w=w: nc.sync.dma_start(w_qkv[:, i * D:(i + 1) * D], w).then_inc(s_w, 16))
        for i, v in enumerate((bq, bk, bv, bo)):
            sp.do(lambda i=i, v=v: nc.sync.dma_start(
                bias_row[:, i * D:(i + 1) * D], v.rearrange("(a d) -> a d", a=1)).then_inc(s_w, 16))
        sp.do(lambda: nc.sync.dma_start(xt, x_t).then_inc(s_xt, 16))
        sp.do(lambda: nc.sync.dma_start(w_o[:, :], Wo).then_inc(s_w, 16))
        sp.do(lambda: nc.sync.dma_start(w_e[0:EF, :], We).then_inc(s_w, 16))
        sp.do(lambda: nc.sync.dma_start(w_e[EF:EF + 1, :], be.rearrange("(a h) -> a h", a=1))
              .then_inc(s_w, 16))
        for b in range(NB):
            sp.wait("staged", b)
            sp.do(lambda b=b: nc.sync.dma_start(
                kv_table[b * P:b * P + rows(b), :], kv_stage[0:rows(b), b % STAGES, :])
                .then_inc(s_table[b % STAGES], 16))

        first = [None]

        def load_indices(b):
            i = b % 2
            if b == 0:
                sp.wait_dma(s_row, 16)
                sp.wait("x zero")
            if b >= 2:
                sp.wait_dma(*kv_ready(b - 2, G - 1))
                sp.wait("shifted", b - 2)

            def read_start():
                first[0] = nc.sync.value_load(start_row[0:1, b:b + 1], min_val=0, max_val=E - C)
            sp.do(read_start)
            for to, frm, s in ((src_i, src, s_src), (dst_i, dst, s_dst)):
                sp.do(lambda to=to, frm=frm, s=s: nc.sync.dma_start(
                    to[:, i, :], frm[bass.ds(first[0], C)].rearrange("(p l) -> p l", l=L))
                    .then_inc(s[i], 16))

        def load_edges(b):
            if b >= 2:
                sp.wait("edge terms", b - 2)
            sp.do(lambda: nc.sync.dma_start(edge_f[b % 2][0:EF, :], edge_t[:, bass.ds(first[0], C)])
                  .then_inc(s_edge[b % 2], 16))

        def load_x(b):
            if b >= 2:
                sp.wait("residual", b - 2)
            sp.do(lambda: nc.sync.dma_start(x_blk[0:rows(b), b % 2, :], x[b * P:b * P + rows(b), :])
                  .then_inc(s_x[b % 2], 16))

        def store(b):
            sp.wait("normal", b)
            sp.do(lambda: nc.sync.dma_start(out[b * P:b * P + rows(b), :], y_out[0:rows(b), b % 2, :])
                  .then_inc(s_y[b % 2], 16))

        for b in range(NB + 3):
            if b < NB:
                load_indices(b)
                load_edges(b)
            if 2 <= b < NB + 2:
                load_x(b - 2)
            if b >= 3:
                store(b - 3)
        for i in range(2):
            sp.wait_dma(s_y[i], 16 * len(range(i, NB, 2)))

        block = ctx.enter_context(nc.Block())

        @block.sync
        def _(engine):
            sp.emit(engine)

        @block.gpsimd
        def _(engine):
            pool.emit(engine)

        @block.scalar
        def _(engine):
            act.emit(engine)

        @block.vector
        def _(engine):
            dve.emit(engine)

        @block.tensor
        def _(engine):
            pe.emit(engine)


_INS = ["x", "src", "dst", "L0_gnn_Wq", "L0_gnn_bq", "L0_gnn_Wk", "L0_gnn_bk", "L0_gnn_Wv", "L0_gnn_bv",
        "L0_gnn_We", "L0_gnn_be", "L0_gnn_Wo", "L0_gnn_bo"]


def kernel(**inputs):
    import numpy as _np
    import concourse.bacc as _bacc
    from concourse import mybir as _mybir
    from concourse.bass_utils import run_bass_kernel_spmd as _run

    nc = _bacc.Bacc("TRN2", target_bir_lowering=False, num_devices=1)
    host = {name: _np.ascontiguousarray(inputs[name]) for name in _INS}
    host["x_t"] = _np.ascontiguousarray(_np.asarray(inputs["x"]).T)
    host["edge_t"] = _np.ascontiguousarray(_np.asarray(inputs["edge_attr_64"]).T)
    arrays, args = {}, {}
    for name, a in host.items():
        arrays[f"in_{name}"] = a
        args[name.replace("L0_gnn_", "")] = nc.dram_tensor(
            f"in_{name}", a.shape, _mybir.dt.from_np(a.dtype), kind="ExternalInput").ap()
    out = nc.dram_tensor("out_0", host["x"].shape, _mybir.dt.float32, kind="ExternalOutput").ap()
    graph_attention(nc, out=out, **args)
    r = _run(nc, [arrays], core_ids=[0])
    return r.results[0]["out_0"]
```

```python
from contextlib import ExitStack

import concourse.bass as bass
from concourse import mybir

P = 128
F32 = mybir.dt.float32
I32 = mybir.dt.int32
ALU = mybir.AluOpType
ACT = mybir.ActivationFunctionType
AX = mybir.AxisListType

QUAD = 4
FAR = -3.0e38
LN_EPS = 1e-5
DEN_EPS = 1e-10


class Line:

    def __init__(self, marks, semaphore):
        self.marks, self.semaphore, self.count, self.items = marks, semaphore, 0, []

    def do(self, emit, mark=None):
        if mark is not None:
            mark = mark if isinstance(mark, tuple) else (mark,)
            self.count += 1
            assert mark not in self.marks, mark
            self.marks[mark] = (self, self.count)
        self.items.append(("do", emit, mark))

    def wait(self, *mark):
        self.items.append(("wait", mark, None))

    def wait_dma(self, semaphore, value):
        self.items.append(("dma", semaphore, value))

    def split(self):
        before = Line(self.marks, self.semaphore)
        before.items, self.items = self.items, []
        return before

    def emit(self, engine, round_=None, passed=None):
        for kind, a, b in self.items:
            if kind == "dma":
                if round_ is None:
                    engine.wait_ge(a, b)
                else:
                    engine.wait_ge(a, round_ * b + b)
                    engine.sem_inc(passed)
            elif kind == "wait":
                line, count = self.marks[a]
                if round_ is None:
                    engine.wait_ge(line.semaphore, count)
                else:
                    engine.wait_ge(line.semaphore, round_ * line.count + count)
                    engine.sem_inc(passed)
            else:
                instruction = a()
                if b is not None:
                    instruction.then_inc(self.semaphore, 1)


def graph_attention(nc, x, x_t, src, dst, edge_t, Wq, bq, Wk, bk, Wv, bv, We, be, Wo, bo, out):
    N, D = x.shape
    E = src.shape[0]
    EF, H = We.shape
    HD = D // H
    NB = -(-N // P)
    SLACK = 4 * int((P * E / N) ** 0.5)
    L = -(-(P * E // N + SLACK) // P)
    C = P * L
    G = -(-L // QUAD)
    STEP = [(g * QUAD, min(L, g * QUAD + QUAD)) for g in range(G)]
    SCALE = float(HD) ** -0.5
    RP = max(r for r in range(1, P) if E % r == 0)
    RC = E // RP
    GP, NCH = RP, RC
    NS = NB + 1
    LAST = N - (NB - 1) * P
    KV, QKV = 2 * D, 3 * D
    WV = D + H
    STAGES = 4
    LAG = 4
    AHEAD = 2

    ctx = ExitStack()
    with ctx:
        def sb(name, shape, dt=F32):
            return ctx.enter_context(nc.sbuf_tensor(name, shape, dt))

        def ps(name, shape):
            return ctx.enter_context(nc.psum_tensor(name, shape, F32))

        def sem(name):
            return ctx.enter_context(nc.semaphore(name))

        kv_table = nc.dram_tensor("kv_table", [N, KV], F32).ap()

        ident = sb("ident", [P, P])
        iota_i = sb("iota_i", [P, P], I32)
        iota_n = sb("iota_n", [P, P])
        ones = sb("ones", [P, P])
        w_qkv = sb("w_qkv", [P, QKV])
        w_o = sb("w_o", [P, D])
        w_e = sb("w_e", [EF + 1, H])
        bias_bc = sb("bias_bc", [P, QKV + D])
        q_all = sb("q_all", [P, NB, D])
        kv_buf = sb("kv_buf", [P, 2, L, KV])
        onehot = sb("onehot", [P, 2, L, P])
        onehot_t = sb("onehot_t", [P, 2, QUAD * P])
        bias_row = onehot_t[0:1, 0, 0:QKV + D]
        edge_f = [sb(f"edge_f{i}", [EF + 1, C]) for i in range(2)]
        src_i = sb("src_i", [P, 2, L], I32)
        dst_i = sb("dst_i", [P, 2, L], I32)
        dst_f = sb("dst_f", [P, 2, L])
        neg_rel = sb("neg_rel", [P, 2, L])
        distance = sb("distance", [P, 2, QUAD * P])
        prod = sb("prod", [P, 2, QUAD * D])
        score = sb("score", [P, 2, H, L])
        run_fwd = sb("run_fwd", [P, H * L])
        shifted = run_fwd[:, :].rearrange("p (h t) -> p h t", h=H)
        run_max = sb("run_max", [P, H, L])
        end_fwd = sb("end_fwd", [P, H, L])
        end_bwd = sb("end_bwd", [P, H, L])
        not_first = sb("not_first", [P, L])
        not_last = sb("not_last", [P, L])
        run_far = sb("run_far", [P, L])
        cand = sb("cand", [P, 2, H, L])
        ends = sb("ends", [P, 4, H])
        seq_val = sb("seq_val", [H, 2 * P])
        seq_dst = sb("seq_dst", [H, 2 * P])
        seq_ef = sb("seq_ef", [H, 2 * P])
        seq_eb = sb("seq_eb", [H, 2 * P])
        seq_ne = sb("seq_ne", [H, 2 * P])
        seq_f = sb("seq_f", [H, 2 * P])
        seq_b = sb("seq_b", [H, 2 * P])
        weight = sb("weight", [P, 2, H, L])
        wv = sb("wv", [P, 2, QUAD, WV])
        den = sb("den", [P, H])
        rec = sb("rec", [P, H])
        agg_n = sb("agg_n", [P, D])
        y_sum = sb("y_sum", [P, D])
        agg_t = sb("agg_t", [P, D])
        x_blk = sb("x_blk", [P, 2, D])
        stats = sb("stats", [P, 6])
        moments = sb("moments", [P, 2])
        rstd = sb("rstd", [P, 2])
        eps_c = sb("eps_c", [P, 1])
        y_out = sb("y_out", [P, 2, D])
        xt = onehot[:, :, :, :].rearrange("p a l n -> p (a l n)")[:, 0:N]
        kv_stage = kv_buf[:, 0, 0:2 * STAGES, :].rearrange("p (s a) d -> p s a d", a=2)
        dst2d_i = kv_buf[0:RP, 0, 8:8 + -(-RC // KV), :].rearrange("p a b -> p (a b)")[:, 0:RC].bitcast(I32)
        row_i = kv_buf[0:NS, 0, 16:16 + -(-RC // KV), :].rearrange("p a b -> p (a b)")[:, 0:RC].bitcast(I32)
        sort_f = kv_buf[0:RP, 0, 24:24 + -(-RC // KV), :].rearrange("p a b -> p (a b)")[:, 0:RC - 1]
        row_f = kv_buf[0:NS, 0, 16:16 + -(-RC // KV), :].rearrange("p a b -> p (a b)")[:, 0:RC]
        assert 24 + -(-RC // KV) <= L and 8 * KV >= RC and 2 * STAGES <= 8 and 2 * L * P >= N
        def over_kv(parts, slot, n, at=0):
            return kv_buf[0:parts, 1, slot:slot + -(-n // KV), :].rearrange("p a b -> p (a b)")[:, at:at + n]

        assert L > 15 and 2 * P <= KV and H * P <= 4 * KV
        g_kv = over_kv(GP, 0, KV)
        g_spread = over_kv(GP, 1, H * P)
        g_z = over_kv(P, 5, H * GP)
        g_wv = over_kv(GP, 9, WV)
        g_acc = over_kv(P, 10, WV)
        g_hot = over_kv(GP, 11, P)
        g_hot_t = over_kv(P, 12, GP)
        g_mask = over_kv(P, 12, GP, P)
        g_prod = over_kv(GP, 13, D)
        g_score, g_in, g_far, g_dst_f, g_shift, g_shift2 = (
            over_kv(GP, 14, n, at) for n, at in ((H, 0), (1, 8), (1, 9), (1, 10), (H, 16), (H, 24)))
        g_base, g_max, g_new, g_zmax, g_drop, g_keep = (
            over_kv(P, 14, n, at) for n, at in ((1, 64), (H, 72), (H, 80), (H, 88), (H, 96), (H, 104)))
        g_src, g_dst = (over_kv(GP, 15, 1, at).bitcast(I32) for at in (0, 1))
        g_edge = edge_f[0][:, 0:GP]
        border_i = sb("border_i", [P, NS], I32)
        border = sb("border", [P, NS])
        border_p = sb("border_p", [P, 1])
        border_pi = sb("border_pi", [P, 1], I32)
        last_f = sb("last_f", [P, 1])
        below = sb("below", [P, NS])
        rows_f = sb("rows_f", [P, 1])
        rows_i = sb("rows_i", [P, 1], I32)
        cnt = sb("cnt", [P, 1])
        start_f = sb("start_f", [P, 1])
        first_f = sb("first_f", [P, 1])
        falls = sb("falls", [P, 1])
        row_s = prod[0:1, 0, 0:3 * P]
        row_x = prod[0:1, 1, 0:2 * P]
        row_b = prod[0:1, 1, 2 * P:2 * P + NS]
        sorted_f = sb("sorted_f", [1, 8])
        lo_row = sb("lo_row", [1, NS], I32)
        hi_row = sb("hi_row", [1, NS], I32)
        general_i = sb("general_i", [1, 1], I32)
        start_row = sb("start_row", [1, NS], I32)

        ps_t = [ps(f"ps_t{i}", [P, 512]) for i in range(2)]
        ps_q = [ps(f"ps_q{i}", [P, 512]) for i in range(2)]
        ps_e = ps("ps_e", [P, 512])
        ps_a = [ps(f"ps_a{i}", [P, 512]) for i in range(2)]
        ps_s = ps("ps_s", [P, 512])

        back_max = ps_s[:, 0:2 * H]
        assert L * H <= 512

        def sums(b):
            return ps_a[b % 2][:, 0:WV]

        def turned(b):
            return ps_a[b % 2][:, WV:WV + D]

        def projected(b):
            return ps_a[b % 2][:, WV + D:WV + 2 * D]

        s_wkv, s_bias, s_wrest = sem("s_wkv"), sem("s_bias"), sem("s_wrest")
        s_xt = [sem(f"s_xt{i}") for i in range(min(4, NB))]
        s_dst2d = sem("s_dst2d")
        s_rows = sem("s_rows")
        s_table = [sem(f"s_table{i}") for i in range(STAGES)]
        s_src = [sem(f"s_src{i}") for i in range(2)]
        s_dst = [sem(f"s_dst{i}") for i in range(2)]
        s_edge = [sem(f"s_edge{i}") for i in range(2)]
        s_x = [sem(f"s_x{i}") for i in range(2)]
        s_kv = [[sem(f"s_kv{i}_{g}") for g in range(G)] for i in range(2)]
        s_y = [sem(f"s_y{i}") for i in range(2)]
        marks = {}
        pool, act, dve, pe = (Line(marks, sem(f"s_{n}")) for n in ("pool", "act", "dve", "pe"))
        sp = Line(marks, None)
        V, T, S = nc.vector, nc.tensor, nc.scalar

        def kv_ready(b, g):
            return s_kv[b % 2][g], 16 * (STEP[g][1] - STEP[g][0]) * (b // 2 + 1)

        def rows(b):
            return P if b < NB - 1 else LAST

        for i, v in enumerate((bq, bk, bv, bo)):
            act.do(lambda i=i, v=v: nc.scalar.dma_start(
                bias_row[:, i * D:(i + 1) * D], v.rearrange("(a d) -> a d", a=1)).then_inc(s_bias, 16))
        act.do(lambda: nc.scalar.dma_start(dst2d_i, dst.rearrange("(r c) -> r c", c=RC))
               .then_inc(s_dst2d, 16))
        pool.do(lambda: nc.gpsimd.memset(ident[:, :], 0.0), "ident zero")
        pool.do(lambda: nc.gpsimd.iota(iota_i[:, :], [[1, P]], base=0, channel_multiplier=0))
        pool.do(lambda: nc.gpsimd.iota(border_i[:, :], [[P, NS]], base=0, channel_multiplier=0))
        pool.do(lambda: nc.gpsimd.iota(border_pi[:, :], [[0, 1]], base=0, channel_multiplier=P), "iotas")
        pool.wait("ident zero")
        pool.do(lambda: nc.gpsimd.affine_select(
            out=ident[:, :], in_=ident[:, :], compare_op=ALU.not_equal, fill=1.0, base=0,
            pattern=[[-1, P]], channel_multiplier=1), "ident")

        pool.wait("ident")
        for i in range(2):
            pool.do(lambda i=i: nc.gpsimd.memset(edge_f[i][EF:EF + 1, :], 1.0), ("edge ones", i))

        dve.do(lambda: V.memset(ones[:, :], 1.0), "ones")
        dve.do(lambda: V.memset(eps_c[:, :], LN_EPS))
        dve.do(lambda: V.memset(x_blk[:, :, :], 0.0), "x zero")
        dve.wait("iotas")
        dve.do(lambda: V.tensor_copy(iota_n[:, :], iota_i[:, :]), "iota_n")
        dve.do(lambda: V.tensor_copy(border[:, :], border_i[:, :]))
        dve.do(lambda: V.tensor_copy(border_p[:, :], border_pi[:, :]))

        dve.wait_dma(s_dst2d, 16)
        dve.do(lambda: V.tensor_copy(last_f[0:RP, :], dst2d_i[:, RC - 1:RC]), "row last")
        dve.wait("row last")
        dve.do(lambda: V.tensor_scalar(below[0:RP, :], border[0:RP, :], last_f[0:RP, 0:1], None,
                                       ALU.is_gt), "rows below")
        pe.wait("rows below")
        pe.do(lambda: T.matmul(ps_s[0:NS, 0:1], below[0:RP, :], ones[0:RP, 0:1],
                               start=True, stop=True), "rows counted")
        dve.wait("rows counted")
        dve.do(lambda: V.tensor_scalar(rows_f[0:NS, :], ps_s[0:NS, 0:1], float(RP - 1), None,
                                       ALU.min), "border row")
        dve.wait("border row")
        dve.do(lambda: V.tensor_copy(rows_i[0:NS, :], rows_f[0:NS, :]), "border row int")
        pool.wait("border row int")
        pool.do(lambda: nc.gpsimd.indirect_dma_start(
            row_i, None, dst.rearrange("(r c) -> r c", c=RC),
            bass.IndirectOffsetOnAxis(ap=rows_i[0:NS, 0:1], axis=0)).then_inc(s_rows, 16))

        pe.wait("ones")
        pe.wait_dma(s_bias, 64)
        pe.do(lambda: T.matmul(ps_e[:, 0:QKV + D], ones[0:1, :], bias_row[:, :],
                               start=True, stop=True), "bias spread")
        dve.wait("bias spread")
        dve.do(lambda: V.tensor_copy(bias_bc[:, :], ps_e[:, 0:QKV + D]), "bias")

        banks = (ps_q[0], ps_q[1], ps_t[0], ps_t[1])

        def in_groups(n):
            return [(b, min(n, NB - 1 - b)) for b in range(0, NB - 1, n)] + [(NB - 1, 1)]

        def bias_of(lo, hi, n, count):
            return bias_bc[0:n, lo:hi].rearrange("p (a d) -> p a d", a=1).to_broadcast([n, count, hi - lo])

        KV_GROUPS = in_groups(2)
        Q_GROUPS = in_groups(4)
        xt_blocks = -(-NB // len(s_xt))

        pe.wait_dma(s_wkv, 32)
        dve.wait("bias")

        def project_kv(j):
            b, count = KV_GROUPS[j]
            n, bank = rows(b), banks[j % 4]
            if j >= 4:
                pe.wait("staged", j - 4)
            for k in range(b, b + count):
                if k % xt_blocks == 0:
                    pe.wait_dma(s_xt[k // xt_blocks], 16)
                pe.do(lambda k=k: T.matmul(bank[0:n, (k - b) * KV:(k - b + 1) * KV],
                                           xt[:, k * P:k * P + n], w_qkv[:, D:QKV],
                                           start=True, stop=True),
                      ("projected kv", j) if k == b + count - 1 else None)
            dve.wait("projected kv", j)
            if j >= STAGES:
                dve.wait_dma(s_table[j % STAGES], 16 * (j // STAGES))
            dve.do(lambda: V.tensor_tensor(
                kv_stage[0:n, j % STAGES, 0:count, :],
                bank[0:n, 0:count * KV].rearrange("p (a d) -> p a d", a=count),
                bias_of(D, QKV, n, count), ALU.add), ("staged", j))

        def project_q(j):
            b, count = Q_GROUPS[j]
            n, bank = rows(b), banks[j % 4]
            if j < 4:
                pe.wait("staged", len(KV_GROUPS) - 1)
            else:
                pe.wait("q", j - 4)
            for k in range(b, b + count):
                pe.do(lambda k=k: T.matmul(bank[0:n, (k - b) * D:(k - b + 1) * D],
                                           xt[:, k * P:k * P + n], w_qkv[:, 0:D], start=True, stop=True),
                      ("projected q", j) if k == b + count - 1 else None)
            dve.wait("projected q", j)
            dve.do(lambda: V.tensor_tensor(
                q_all[0:n, b:b + count, :],
                bank[0:n, 0:count * D].rearrange("p (a d) -> p a d", a=count),
                bias_of(0, D, n, count), ALU.add), ("q", j))

        def find_windows():
            dve.wait_dma(s_rows, 16)
            dve.do(lambda: V.tensor_copy(row_f, row_i), "row")
            dve.wait("row")
            dve.do(lambda: V.tensor_scalar(row_f, row_f, border_p[0:NS, 0:1], None, ALU.is_lt), "row below")
            dve.wait("row below")
            dve.do(lambda: V.tensor_reduce(cnt[0:NS, :], row_f, AX.X, ALU.add), "row count")
            dve.wait("row count")
            dve.do(lambda: V.scalar_tensor_tensor(
                out=start_f[0:NS, 0:1], in0=rows_f[0:NS, :], scalar=float(RC), in1=cnt[0:NS, :],
                op0=ALU.mult, op1=ALU.add), "border edge")
            dve.wait("border edge")
            pe.wait("border edge")
            pe.wait("ident")
            pe.do(lambda: T.transpose(ps_s[0:1, 0:NS], start_f[0:NS, 0:1], ident[0:NS, 0:NS]))
            dve.do(lambda: V.tensor_tensor(sort_f, dst2d_i[:, 1:RC], dst2d_i[:, 0:RC - 1], ALU.is_lt), "falls")
            dve.do(lambda: V.tensor_copy(first_f[0:RP, :], dst2d_i[:, 0:1]))
            dve.wait("falls")
            dve.do(lambda: V.tensor_reduce(falls[0:RP, :], sort_f, AX.X, ALU.add), "falls by row")
            pe.wait("falls by row")
            pe.do(lambda: T.matmul(ps_s[0:1, NS:NS + 1], falls[0:RP, :], ones[0:RP, 0:1], start=True,
                                   stop=True))
            pe.do(lambda: T.transpose(ps_s[0:1, P:P + RP], first_f[0:RP, :], ident[0:RP, 0:RP]))
            pe.do(lambda: T.transpose(ps_s[0:1, 2 * P:2 * P + RP], last_f[0:RP, :], ident[0:RP, 0:RP]),
                  "rows turned")
            dve.wait("rows turned")
            dve.do(lambda: V.tensor_copy(row_s[:, 0:NS + 1], ps_s[0:1, 0:NS + 1]))
            dve.do(lambda: V.tensor_copy(row_s[:, P:P + RP], ps_s[0:1, P:P + RP]))
            dve.do(lambda: V.tensor_copy(row_s[:, 2 * P:2 * P + RP], ps_s[0:1, 2 * P:2 * P + RP]), "row s")
            dve.wait("row s")
            borders = row_s[:, 0:NS]
            dve.do(lambda: V.tensor_tensor(row_x[:, 0:RP - 1], row_s[:, P + 1:P + RP],
                                           row_s[:, 2 * P:2 * P + RP - 1], ALU.is_lt), "row falls")
            dve.do(lambda: V.tensor_scalar(row_b[:, :], borders, float(E - C), None, ALU.min), "start")
            dve.wait("row falls")
            dve.do(lambda: V.tensor_reduce(sorted_f[:, 0:1], row_x[:, 0:RP - 1], AX.X, ALU.add), "x falls")
            dve.wait("start")
            dve.do(lambda: V.tensor_copy(start_row[:, :], row_b[:, :]), "starts")
            dve.do(lambda: V.tensor_tensor(row_x[:, P:P + NB], row_s[:, 1:NS], row_b[:, 0:NB], ALU.subtract),
                   "needed")
            dve.wait("needed")
            dve.do(lambda: V.tensor_scalar(row_x[:, P:P + NB], row_x[:, P:P + NB], float(C), None,
                                           ALU.is_gt), "over")
            dve.wait("over")
            dve.do(lambda: V.tensor_reduce(sorted_f[:, 1:2], row_x[:, P:P + NB], AX.X, ALU.add))
            dve.wait("x falls")
            dve.do(lambda: V.tensor_tensor(sorted_f[:, 2:3], sorted_f[:, 0:1], row_s[:, NS:NS + 1], ALU.add),
                   "unsorted")
            dve.wait("unsorted")
            dve.do(lambda: V.tensor_tensor(sorted_f[:, 3:4], sorted_f[:, 1:2], sorted_f[:, 2:3], ALU.add),
                   "general f")
            dve.do(lambda: V.tensor_scalar(sorted_f[:, 4:5], sorted_f[:, 2:3], 1.0, 4.0 * NCH, ALU.min,
                                           ALU.mult), "everything")
            dve.do(lambda: V.tensor_scalar(row_x[:, 0:NS], borders, 1.0 / GP, None, ALU.mult), "chunk f")
            dve.wait("chunk f")
            dve.do(lambda: V.tensor_scalar(row_b[:, :], row_x[:, 0:NS], -1.0, sorted_f[:, 4:5], ALU.add,
                                           ALU.subtract), "lo f")
            dve.wait("lo f")
            dve.do(lambda: V.tensor_scalar(lo_row[:, :], row_b[:, :], 0.0, None, ALU.max), "lo")
            dve.wait("lo")
            dve.do(lambda: V.tensor_scalar(row_b[:, :], row_x[:, 0:NS], 1.0, sorted_f[:, 4:5], ALU.add,
                                           ALU.add), "hi f")
            dve.wait("hi f")
            dve.do(lambda: V.tensor_scalar(hi_row[:, :], row_b[:, :], float(NCH), None, ALU.min), "hi")
            dve.do(lambda: V.tensor_copy(general_i[:, :], sorted_f[:, 3:4]), "general")

        for j in range(len(KV_GROUPS)):
            project_kv(j)
            if j == min(9, len(KV_GROUPS) - 1):
                find_windows()
        dve.do(lambda: V.memset(q_all[:, NB - 1, :], 0.0), "q zero")
        dve.wait_dma(s_wrest, 64)
        dve.do(lambda: V.tensor_scalar(w_qkv[:, 0:D], w_qkv[:, 0:D], SCALE, None, ALU.mult))
        dve.do(lambda: V.tensor_scalar(bias_bc[:, 0:D], bias_bc[:, 0:D], SCALE, None, ALU.mult), "scaled")
        dve.wait("scaled")
        dve.wait("q zero")
        pe.wait("scaled")
        for j in range(len(Q_GROUPS)):
            project_q(j)
        for line in (pe, act):
            line.wait("q", len(Q_GROUPS) - 1)

        for i in range(STAGES):
            pool.wait_dma(s_table[i], 16 * len(range(i, len(KV_GROUPS), STAGES)))

        pe.wait("edge ones", 1)
        act.wait("x zero")
        pool_first, act_first, dve_first, pe_first = (
            line.split() for line in (pool, act, dve, pe))
        for b in range(NB):
            pool.wait_dma(s_src[b % 2], 16 * (b // 2 + 1))
            for g, (t0, t1) in enumerate(STEP):
                if b >= 2:
                    pool.wait("weighted", (b - 2) * G + g)
                for t in range(t0, t1):
                    pool.do(lambda b=b, t=t, g=g: nc.gpsimd.indirect_dma_start(
                        kv_buf[:, b % 2, t, :], None, kv_table,
                        bass.IndirectOffsetOnAxis(ap=src_i[:, b % 2, t:t + 1], axis=0))
                        .then_inc(s_kv[b % 2][g], 16))

        def indices(b):
            i = b % 2
            dve.wait_dma(s_dst[i], 16 * (b // 2 + 1))
            dve.do(lambda: V.tensor_copy(dst_f[:, i, :], dst_i[:, i, :]), ("dst", b))
            dve.wait("dst", b)
            if b >= 2:
                dve.wait("onehot", (b - 1) * G - 1)
            dve.do(lambda: V.tensor_scalar(neg_rel[:, i, :], dst_f[:, i, :], -1.0, float(P * b),
                                           ALU.mult, ALU.add), ("dst rel", b))

        def multiply(q):
            b, (t0, t1) = q // G, STEP[q % G]
            n = t1 - t0
            dve.wait("q by edge", q)
            dve.wait_dma(*kv_ready(b, q % G))
            if q >= 2:
                dve.wait("dot", q - 2)
            dve.do(lambda: V.tensor_tensor(
                prod[:, q % 2, 0:n * D].rearrange("p (t d) -> p t d", d=D),
                ps_q[q % 2][:, 0:n * D].rearrange("p (t d) -> p t d", d=D),
                kv_buf[:, b % 2, t0:t1, 0:D], ALU.mult), ("product", q))

        def dot(q):
            b, (t0, t1) = q // G, STEP[q % G]
            dve.wait("product", q)
            dve.do(lambda: V.tensor_reduce(
                score[:, b % 2, :, t0:t1].rearrange("p h t -> p t h"),
                prod[:, q % 2, 0:(t1 - t0) * D].rearrange("p (t h d) -> p t h d", h=H, d=HD),
                AX.X, ALU.add), ("dot", q))

        def weigh(q):
            b, (t0, t1) = q // G, STEP[q % G]
            dve.wait("weights", b)
            if q >= 2:
                dve.wait("summed", q - 2)
            dve.do(lambda: V.tensor_tensor(
                wv[:, q % 2, 0:t1 - t0, 0:D].rearrange("p t (h d) -> p t h d", d=HD),
                kv_buf[:, b % 2, t0:t1, D:KV].rearrange("p t (h d) -> p t h d", d=HD),
                weight[:, b % 2, :, t0:t1].rearrange("p h (t a) -> p t h a", a=1)
                .to_broadcast([P, t1 - t0, H, HD]), ALU.mult), ("weighted", q))

        def flat(a):
            return a.rearrange("p h t -> p (h t)")

        def per_edge(a, n):
            return a.rearrange("p (a t) -> p a t", a=1).to_broadcast([P, H, n])

        def by_end(a):
            return a.rearrange("h (p e) -> h e p", e=2)

        def run_maxima(b):
            i = b % 2
            d = dst_f[:, i, :]
            s = score[:, i, :, :]
            dve.wait("edge terms", b)
            dve.wait("dot", (b + 1) * G - 1)
            dve.do(lambda: V.tensor_tensor(s, s, ps_e[:, 0:L * H].rearrange("p (t h) -> p h t", h=H),
                                           ALU.add), ("score", b))
            dve.do(lambda: V.memset(end_fwd[:, :, 0:1], FAR))
            dve.do(lambda: V.memset(end_bwd[:, :, L - 1:L], FAR))
            dve.do(lambda: V.tensor_tensor(run_far[:, 1:L], d[:, 1:L], d[:, 0:L - 1], ALU.not_equal),
                   ("changes", b))
            dve.wait("changes", b)
            dve.do(lambda: V.tensor_scalar(end_fwd[:, :, 1:L], per_edge(run_far[:, 1:L], L - 1), FAR,
                                           None, ALU.mult))
            dve.do(lambda: V.tensor_scalar(end_bwd[:, :, 0:L - 1], per_edge(run_far[:, 1:L], L - 1),
                                           FAR, None, ALU.mult), ("run ends", b))
            dve.wait("run ends", b)
            if b >= 1:
                dve.wait("weights", b - 1)
            dve.do(lambda: V.tensor_tensor_scan(run_fwd[:, :], flat(end_fwd[:, :, :]), flat(s), FAR,
                                                ALU.add, ALU.max), ("forward", b))
            dve.wait("forward", b)
            dve.do(lambda: V.tensor_tensor_scan(
                flat(run_max[:, :, :])[:, ::-1], flat(end_bwd[:, :, :])[:, ::-1], run_fwd[:, ::-1],
                FAR, ALU.add, ALU.max), ("backward", b))
            dve.wait("backward", b)
            dve.do(lambda: V.tensor_copy(ends[:, 0, :], run_max[:, :, 0]))
            dve.do(lambda: V.tensor_copy(ends[:, 1, :], run_max[:, :, L - 1]))
            dve.do(lambda: V.tensor_copy(ends[:, 2, :], d[:, 0:1].to_broadcast([P, H])))
            dve.do(lambda: V.tensor_copy(ends[:, 3, :], d[:, L - 1:L].to_broadcast([P, H])), ("ends", b))
            dve.do(lambda: V.tensor_scalar(not_first[:, :], d, d[:, 0:1], FAR, ALU.not_equal, ALU.mult))
            dve.do(lambda: V.tensor_scalar(not_last[:, :], d, d[:, L - 1:L], FAR, ALU.not_equal,
                                           ALU.mult), ("away", b))

        def turn_ends(b):
            pe.wait("ends", b)
            if b >= 1:
                pe.wait("candidates", b - 1)
            for k in range(4):
                pe.do(lambda k=k: T.transpose(ps_s[0:H, k * P:(k + 1) * P], ends[:, k, :], ident[:, :]),
                      ("ends turned", b) if k == 3 else None)

        def crossing_maxima(b):
            dve.wait("ends turned", b)
            dve.do(lambda: V.tensor_copy(by_end(seq_val[:, :]),
                                         ps_s[0:H, 0:2 * P].rearrange("h (e p) -> h e p", e=2)))
            dve.do(lambda: V.tensor_copy(by_end(seq_dst[:, :]),
                                         ps_s[0:H, 2 * P:4 * P].rearrange("h (e p) -> h e p", e=2)),
                   ("sequence", b))
            dve.wait("sequence", b)
            dve.do(lambda: V.memset(seq_ef[:, 0:1], FAR))
            dve.do(lambda: V.memset(seq_eb[:, 2 * P - 1:2 * P], FAR))
            dve.do(lambda: V.tensor_tensor(seq_ne[:, 1:2 * P], seq_dst[:, 1:2 * P],
                                           seq_dst[:, 0:2 * P - 1], ALU.not_equal), ("seq changes", b))
            dve.wait("seq changes", b)
            dve.do(lambda: V.tensor_scalar(seq_ef[:, 1:2 * P], seq_ne[:, 1:2 * P], FAR, None, ALU.mult))
            dve.do(lambda: V.tensor_scalar(seq_eb[:, 0:2 * P - 1], seq_ne[:, 1:2 * P], FAR, None,
                                           ALU.mult), ("seq ends", b))
            dve.wait("seq ends", b)
            dve.do(lambda: V.tensor_tensor_scan(seq_f[:, :], seq_ef[:, :], seq_val[:, :], FAR, ALU.add,
                                                ALU.max), ("seq forward", b))
            dve.wait("seq forward", b)
            dve.do(lambda: V.tensor_tensor_scan(seq_b[:, ::-1], seq_eb[:, ::-1], seq_f[:, ::-1], FAR,
                                                ALU.add, ALU.max), ("seq backward", b))

        def turn_crossing(b):
            pe.wait("seq backward", b)
            for k in range(2):
                pe.do(lambda k=k: T.transpose(
                    back_max[:, k * H:(k + 1) * H], seq_b[:, :].rearrange("h (p e) -> h p e", e=2)[:, :, k],
                    ident[0:H, 0:H]), ("crossing", b) if k == 1 else None)

        def edge_maxima(b):
            s = score[:, b % 2, :, :]
            dve.wait("crossing", b)
            for k, away in enumerate((not_first, not_last)):
                dve.do(lambda k=k, away=away: V.tensor_tensor(
                    cand[:, k, :, :],
                    back_max[:, k * H:(k + 1) * H].rearrange("p (h a) -> p h a", a=1).to_broadcast([P, H, L]),
                    per_edge(away[:, :], L), ALU.add), ("candidates", b) if k == 1 else None)
            dve.wait("candidates", b)
            dve.do(lambda: V.tensor_tensor(cand[:, 0, :, :], cand[:, 0, :, :], cand[:, 1, :, :], ALU.max),
                   ("larger", b))
            dve.wait("larger", b)
            dve.do(lambda: V.tensor_tensor(run_max[:, :, :], run_max[:, :, :], cand[:, 0, :, :], ALU.max),
                   ("maximum", b))
            dve.wait("maximum", b)
            dve.do(lambda: V.tensor_tensor(shifted[:, :, :], s, run_max[:, :, :], ALU.subtract),
                   ("shifted", b))

        def divide(b):
            dve.wait("summed", (b + 1) * G - 1)
            dve.do(lambda: V.tensor_scalar(den[:, :], sums(b)[:, D:WV], DEN_EPS, None, ALU.add), ("den", b))
            dve.wait("den", b)
            dve.do(lambda: V.reciprocal(rec[:, :], den[:, :]), ("rec", b))
            dve.wait("rec", b)
            if b >= 1:
                dve.wait("aggregate turned", b - 1)
            dve.do(lambda: V.tensor_tensor(
                agg_n[:, :].rearrange("p (h d) -> p h d", d=HD),
                sums(b)[:, 0:D].rearrange("p (h d) -> p h d", d=HD),
                rec[:, :].rearrange("p (h a) -> p h a", a=1).to_broadcast([P, H, HD]), ALU.mult),
                ("aggregate", b))

        def residual(b):
            dve.wait("times Wo", b)
            dve.wait_dma(s_x[b % 2], 16 * (b // 2 + 1))
            dve.do(lambda: V.tensor_tensor(y_sum[:, :], projected(b), x_blk[:, b % 2, :], ALU.add),
                   ("residual", b))
            dve.wait("residual", b)
            dve.do(lambda: V.tensor_tensor(y_sum[:, :], y_sum[:, :], bias_bc[:, QKV:QKV + D], ALU.add),
                   ("y", b))
            dve.wait("y", b)
            dve.do(lambda: V.bn_stats(stats[:, :], y_sum[:, :]), ("stats", b))
            dve.wait("stats", b)
            dve.do(lambda: V.bn_aggr(moments[:, :], stats[:, :]), ("moments", b))

        def normalise(b):
            dve.wait("rstd", b)
            if b >= 2:
                dve.wait_dma(s_y[b % 2], 16 * (b // 2))
            dve.do(lambda: V.tensor_scalar(y_out[:, b % 2, :], y_sum[:, :], moments[:, 0:1], rstd[:, 1:2],
                                           ALU.subtract, ALU.mult), ("normal", b))

        def turn_onehot(q):
            b, (t0, t1) = q // G, STEP[q % G]
            pe.wait("onehot", q)
            if q >= 2:
                pe.wait("onehot copied", q - 2)
            for t in range(t0, t1):
                pe.do(lambda t=t: T.transpose(ps_t[q % 2][:, (t - t0) * P:(t - t0 + 1) * P],
                                              onehot[:, b % 2, t, :], ident[:, :]),
                      ("onehot turned", q) if t == t1 - 1 else None)

        def spread_q(q):
            b, (t0, t1) = q // G, STEP[q % G]
            pe.wait("onehot copied", q)
            if q >= 2:
                pe.wait("product", q - 2)
            for t in range(t0, t1):
                pe.do(lambda t=t: T.matmul(
                    ps_q[q % 2][:, (t - t0) * D:(t - t0 + 1) * D],
                    onehot_t[:, q % 2, (t - t0) * P:(t - t0 + 1) * P], q_all[:, b, :],
                    start=True, stop=True), ("q by edge", q) if t == t1 - 1 else None)
            if t0 == 0:
                pe.wait_dma(s_edge[b % 2], 16 * (b // 2 + 1))
                if b >= 1:
                    pe.wait("score", b - 1)
            for t in range(t0, t1):
                pe.do(lambda t=t: T.matmul(ps_e[:, t * H:(t + 1) * H], edge_f[b % 2][:, t:C:L], w_e[:, :],
                                           start=True, stop=True),
                      ("edge terms", b) if t == L - 1 else None)

        def sum_step(q):
            b, (t0, t1) = q // G, STEP[q % G]
            pe.wait("weighted", q)
            pe.wait("weights beside", q)
            if t0 == 0 and b >= 2:
                pe.wait("residual", b - 2)
            for t in range(t0, t1):
                pe.do(lambda t=t: T.matmul(sums(b), onehot[:, b % 2, t, :], wv[:, q % 2, t - t0, :],
                                           start=(t == 0), stop=(t == L - 1)),
                      ("summed", q) if t == t1 - 1 else None)

        def turn_aggregate(b):
            pe.wait("aggregate", b)
            pe.do(lambda: T.transpose(turned(b), agg_n[:, :], ident[:, :]), ("aggregate turned", b))

        def times_wo(b):
            pe.wait("turned copied", b)
            pe.do(lambda: T.matmul(projected(b), agg_t[:, :], w_o[:, :], start=True, stop=True),
                  ("times Wo", b))

        def build_onehot(q):
            b, (t0, t1) = q // G, STEP[q % G]
            act.wait("dst rel", b)
            if q >= 2:
                act.wait("onehot", q - 2)
            for t in range(t0, t1):
                act.do(lambda t=t: S.activation(distance[:, q % 2, (t - t0) * P:(t - t0 + 1) * P], iota_n[:, :],
                                                ACT.Abs, bias=neg_rel[:, b % 2, t:t + 1]),
                       ("distance", q) if t == t1 - 1 else None)
            act.wait("distance", q)
            if b >= 2:
                act.wait("summed", q - 2 * G)
            act.do(lambda: S.activation(
                onehot[:, b % 2, t0:t1, :].rearrange("p t n -> p (t n)"),
                distance[:, q % 2, 0:(t1 - t0) * P], ACT.Relu, bias=1.0, scale=-1.0), ("onehot", q))

        def copy_onehot(q):
            n = (STEP[q % G][1] - STEP[q % G][0]) * P
            act.wait("onehot turned", q)
            if q >= 2:
                act.wait("q by edge", q - 2)
            act.do(lambda: S.copy(onehot_t[:, q % 2, 0:n], ps_t[q % 2][:, 0:n]), ("onehot copied", q))

        def exponentials(b):
            act.wait("shifted", b)
            act.do(lambda: S.activation(weight[:, b % 2, :, :], shifted[:, :, :], ACT.Exp), ("weights", b))

        def copy_weights(q):
            b, (t0, t1) = q // G, STEP[q % G]
            act.wait("weights", b)
            if q >= 2:
                act.wait("summed", q - 2)
            act.do(lambda: S.copy(wv[:, q % 2, 0:t1 - t0, D:WV],
                                  weight[:, b % 2, :, t0:t1].rearrange("p h t -> p t h")),
                   ("weights beside", q))

        def copy_turned(b):
            act.wait("aggregate turned", b)
            if b >= 1:
                act.wait("times Wo", b - 1)
            act.do(lambda: S.copy(agg_t[:, :], turned(b)), ("turned copied", b))

        def inverse_deviation(b):
            act.wait("moments", b)
            act.do(lambda: S.activation(rstd[:, 0:1], moments[:, 1:2], ACT.Ln, bias=eps_c[:, 0:1]),
                   ("log", b))
            act.wait("log", b)
            act.do(lambda: S.activation(rstd[:, 1:2], rstd[:, 0:1], ACT.Exp, scale=-0.5), ("rstd", b))

        indices(0)
        for q in range(AHEAD):
            build_onehot(q)
        for q in range((NB + 2) * G + 8 + LAG):
            b, g = divmod(q, G)
            old = q - G - LAG
            if q < NB * G:
                turn_onehot(q)
                copy_onehot(q)
            if 1 <= q <= NB * G:
                spread_q(q - 1)
            if 1 <= b <= NB:
                if g == 0:
                    run_maxima(b - 1)
                if g == 1:
                    turn_ends(b - 1)
                if g == 3:
                    turn_crossing(b - 1)
            if g == min(4, G - 2) and b + 1 < NB:
                indices(b + 1)
            if q + AHEAD < NB * G:
                build_onehot(q + AHEAD)
            if 0 <= old < NB * G:
                copy_weights(old)
                weigh(old)
            if q < NB * G:
                multiply(q)
            if 1 <= b <= NB:
                if g == 1:
                    crossing_maxima(b - 1)
                if g == 3:
                    edge_maxima(b - 1)
                    exponentials(b - 1)
            if q < NB * G:
                dot(q)
            if 1 <= old <= NB * G:
                sum_step(old - 1)
            for offset, parts in ((1, (divide,)), (2, (turn_aggregate, copy_turned)), (3, (times_wo,)),
                                  (4, (residual,)), (5, (inverse_deviation,)), (7, (normalise,))):
                done, left = divmod(q - 2 * G - LAG - offset, G)
                if 0 <= done < NB and left == 0:
                    for part in parts:
                        part(done)

        for i, w in ((1, Wk), (2, Wv)):
            sp.do(lambda i=i, w=w: nc.sync.dma_start(w_qkv[:, i * D:(i + 1) * D], w).then_inc(s_wkv, 16))
        for k in range(len(s_xt)):
            lo, hi = k * xt_blocks * P, min(N, (k + 1) * xt_blocks * P)
            sp.do(lambda lo=lo, hi=hi, k=k: nc.sync.dma_start(xt[:, lo:hi], x_t[:, lo:hi])
                  .then_inc(s_xt[k], 16))
        sp.do(lambda: nc.sync.dma_start(w_qkv[:, 0:D], Wq).then_inc(s_wrest, 16))
        sp.do(lambda: nc.sync.dma_start(w_o[:, :], Wo).then_inc(s_wrest, 16))
        sp.do(lambda: nc.sync.dma_start(w_e[0:EF, :], We).then_inc(s_wrest, 16))
        sp.do(lambda: nc.sync.dma_start(w_e[EF:EF + 1, :], be.rearrange("(a h) -> a h", a=1))
              .then_inc(s_wrest, 16))
        for j, (b, count) in enumerate(KV_GROUPS):
            sp.wait("staged", j)
            sp.do(lambda j=j, b=b, count=count: nc.sync.dma_start(
                kv_table[b * P:b * P + (count - 1) * P + rows(b), :]
                .rearrange("(a p) d -> p a d", a=count),
                kv_stage[0:rows(b), j % STAGES, 0:count, :])
                .then_inc(s_table[j % STAGES], 16))
        sp.wait("x zero")
        sp_first = sp.split()

        first = [None]

        def load_indices(b):
            i = b % 2
            if b >= 2:
                sp.wait_dma(*kv_ready(b - 2, G - 1))
                sp.wait("dst", b - 2)

            def read_start():
                first[0] = nc.sync.value_load(start_row[0:1, b:b + 1], min_val=0, max_val=E - C)
            sp.do(read_start)
            for to, frm, s in ((src_i, src, s_src), (dst_i, dst, s_dst)):
                sp.do(lambda to=to, frm=frm, s=s: nc.sync.dma_start(
                    to[:, i, :], frm[bass.ds(first[0], C)].rearrange("(p l) -> p l", l=L))
                    .then_inc(s[i], 16))

        def load_edges(b):
            if b >= 2:
                sp.wait("edge terms", b - 2)
            sp.do(lambda: nc.sync.dma_start(edge_f[b % 2][0:EF, :], edge_t[:, bass.ds(first[0], C)])
                  .then_inc(s_edge[b % 2], 16))

        def load_x(b):
            if b >= 2:
                sp.wait("residual", b - 2)
            sp.do(lambda: nc.sync.dma_start(x_blk[0:rows(b), b % 2, :], x[b * P:b * P + rows(b), :])
                  .then_inc(s_x[b % 2], 16))

        def store(b):
            sp.wait("normal", b)
            sp.do(lambda: nc.sync.dma_start(out[b * P:b * P + rows(b), :], y_out[0:rows(b), b % 2, :])
                  .then_inc(s_y[b % 2], 16))

        for b in range(NB + 3):
            if b < NB:
                load_indices(b)
                load_edges(b)
            if 2 <= b < NB + 2:
                load_x(b - 2)
            if b >= 3:
                store(b - 3)
        for i in range(2):
            sp.wait_dma(s_y[i], 16 * len(range(i, NB, 2)))

        lines = {}

        def body(name):
            return {n: Line(lines.setdefault(name, {}), sem(f"s_{name}_{n}"))
                    for n in ("sp", "pool", "act", "dve", "pe")}

        chunk, ended = body("chunk"), body("ended")
        s_gfree = sem("s_gfree")
        s_ginit = sem("s_ginit")
        s_gnode = sem("s_gnode")
        s_gload, s_ggather, s_gx, s_gy = (
            sem(n) for n in ("s_gload", "s_ggather", "s_gx", "s_gy"))
        s_gpad = sem("s_gpad")
        s_passed = {n: sem(f"s_passed_{n}") for n in ("sp", "pool", "act", "dve", "pe")}
        x_pad = nc.dram_tensor("x_pad", [NB * P, D], F32).ap()
        y_pad = nc.dram_tensor("y_pad", [NB * P, D], F32).ap()
        now = {}
        GFAR = -1.0e30

        def heads(a, n, inner):
            return a.rearrange("p (h a) -> p h a", a=1).to_broadcast([n, H, inner])

        def chunk_body():
            sp, pool, act, dve, pe = (chunk[n] for n in ("sp", "pool", "act", "dve", "pe"))
            sp.wait_dma(s_gfree, 1)
            for to, frm in ((g_src, src), (g_dst, dst)):
                sp.do(lambda to=to, frm=frm: nc.sync.dma_start(
                    to, frm[bass.ds(now["chunk"] * GP, GP)].rearrange("(p a) -> p a", a=1))
                    .then_inc(s_gload, 16))
            sp.do(lambda: nc.sync.dma_start(g_edge[0:EF, :], edge_t[:, bass.ds(now["chunk"] * GP, GP)])
                  .then_inc(s_gload, 16))
            pool.wait_dma(s_gload, 48)
            pool.do(lambda: nc.gpsimd.indirect_dma_start(
                g_kv, None, kv_table, bass.IndirectOffsetOnAxis(ap=g_src, axis=0)).then_inc(s_ggather, 16))
            dve.wait_dma(s_gload, 48)
            dve.do(lambda: V.tensor_copy(g_dst_f, g_dst), "dst")
            dve.wait("dst")
            dve.do(lambda: V.tensor_scalar(g_hot, iota_n[0:GP, :], g_base[0:GP, :], g_dst_f, ALU.add,
                                           ALU.is_equal), "hot")
            dve.wait("hot")
            dve.do(lambda: V.tensor_reduce(g_in, g_hot, AX.X, ALU.add), "in")
            dve.wait("in")
            dve.do(lambda: V.tensor_scalar(g_far, g_in, -1.0, -GFAR, ALU.add, ALU.mult))
            pe.wait("hot")
            pe.do(lambda: T.transpose(ps_t[0][:, 0:GP], g_hot, ident[0:GP, 0:GP]), "hot turned")
            act.wait("hot turned")
            act.do(lambda: S.copy(g_hot_t, ps_t[0][:, 0:GP]), "hot copied")
            pe.wait("hot copied")
            pe.wait_dma(s_gload, 48)
            pe.do(lambda: T.matmul(ps_q[0][0:GP, 0:D], g_hot_t, q_all[:, bass.ds(now["block"], 1), :]
                                   .rearrange("p a d -> p (a d)"), start=True, stop=True))
            pe.do(lambda: T.matmul(ps_e[0:GP, 0:H], g_edge, w_e[:, :], start=True, stop=True), "q, edge")
            dve.wait("hot copied")
            dve.do(lambda: V.tensor_scalar(g_mask, g_hot_t, -1.0, -FAR, ALU.add, ALU.mult), "mask")
            dve.wait("q, edge")
            dve.wait_dma(s_ggather, 16)
            dve.do(lambda: V.tensor_tensor(g_prod, ps_q[0][0:GP, 0:D], g_kv[:, 0:D], ALU.mult), "prod")
            dve.wait("prod")
            dve.do(lambda: V.tensor_reduce(g_score, g_prod.rearrange("p (h d) -> p h d", d=HD), AX.X,
                                           ALU.add), "dot")
            dve.wait("dot")
            dve.do(lambda: V.tensor_tensor(g_score, g_score, ps_e[0:GP, 0:H], ALU.add), "score")
            dve.wait("score")
            dve.do(lambda: V.tensor_copy(g_spread.rearrange("p (h n) -> p h n", h=H), heads(g_score, GP, P)),
                   "spread")
            pe.wait("spread")
            half = H // 2
            for h in range(H):
                bank = (ps_s, ps_t[1])[h // half]
                pe.do(lambda h=h, bank=bank: T.matmul(
                    bank[:, (h % half) * GP:(h % half + 1) * GP], g_spread[:, h * P:(h + 1) * P],
                    ident[0:GP, 0:GP], start=True, stop=True), "by node" if h == H - 1 else None)
            dve.wait("by node")
            dve.wait("mask")
            z = g_z.rearrange("p (h e) -> p h e", h=H)
            for k, bank in enumerate((ps_s, ps_t[1])):
                dve.do(lambda k=k, bank=bank: V.tensor_tensor(
                    z[:, k * half:(k + 1) * half, :],
                    bank[:, 0:half * GP].rearrange("p (h e) -> p h e", h=half),
                    g_mask.rearrange("p (a e) -> p a e", a=1).to_broadcast([P, half, GP]), ALU.add),
                    "masked" if k else None)
            dve.wait("masked")
            dve.do(lambda: V.tensor_reduce(g_zmax, z, AX.X, ALU.max), "chunk max")
            dve.wait("chunk max")
            dve.do(lambda: V.tensor_tensor(g_new, g_max, g_zmax, ALU.max), "new max")
            dve.wait("new max")
            dve.do(lambda: V.tensor_tensor(g_drop, g_max, g_new, ALU.subtract), "drop")
            act.wait("drop")
            act.do(lambda: S.activation(g_keep, g_drop, ACT.Exp), "keep")
            pe.wait("new max")
            pe.do(lambda: T.matmul(ps_q[1][0:GP, 0:H], g_hot_t, g_new, start=True, stop=True), "max by edge")
            dve.wait("max by edge")
            dve.do(lambda: V.tensor_tensor(g_shift, g_score, ps_q[1][0:GP, 0:H], ALU.subtract), "shift")
            dve.wait("shift")
            dve.do(lambda: V.tensor_scalar(g_shift2, g_shift, g_far, None, ALU.add), "shift far")
            act.wait("shift far")
            act.do(lambda: S.activation(g_wv[:, D:WV], g_shift2, ACT.Exp), "weight")
            dve.wait("weight")
            dve.do(lambda: V.tensor_tensor(
                g_wv[:, 0:D].rearrange("p (h d) -> p h d", d=HD),
                g_kv[:, D:KV].rearrange("p (h d) -> p h d", d=HD), heads(g_wv[:, D:WV], GP, HD), ALU.mult),
                "weighted")
            pe.wait("weighted")
            pe.do(lambda: T.matmul(ps_a[0][:, 0:WV], g_hot, g_wv, start=True, stop=True), "chunk sums")
            dve.do(lambda: V.tensor_copy(g_max, g_new))
            dve.do(lambda: V.tensor_tensor(
                g_acc[:, 0:D].rearrange("p (h d) -> p h d", d=HD),
                g_acc[:, 0:D].rearrange("p (h d) -> p h d", d=HD), heads(g_keep, P, HD), ALU.mult))
            dve.do(lambda: V.tensor_tensor(g_acc[:, D:WV], g_acc[:, D:WV], g_keep, ALU.mult), "rescaled")
            dve.wait("rescaled")
            dve.wait("chunk sums")
            dve.do(lambda: V.tensor_tensor(g_acc, g_acc, ps_a[0][:, 0:WV], ALU.add), "added")
            dve.wait("added")
            dve.do(lambda: V.nop().then_inc(s_gfree, 1))

        def ended_body():
            sp, pool, act, dve, pe = (ended[n] for n in ("sp", "pool", "act", "dve", "pe"))
            sp.wait_dma(s_gnode, 1)
            sp.do(lambda: nc.sync.dma_start(x_blk[:, 0, :], x_pad[bass.ds(now["block"] * P, P), :])
                  .then_inc(s_gx, 16))
            dve.do(lambda: V.tensor_scalar(den[:, :], g_acc[:, D:WV], DEN_EPS, None, ALU.add), "den")
            dve.wait("den")
            dve.do(lambda: V.reciprocal(rec[:, :], den[:, :]), "rec")
            dve.wait("rec")
            dve.do(lambda: V.tensor_tensor(
                agg_n[:, :].rearrange("p (h d) -> p h d", d=HD),
                g_acc[:, 0:D].rearrange("p (h d) -> p h d", d=HD), heads(rec[:, :], P, HD), ALU.mult),
                "aggregate")
            pe.wait("aggregate")
            pe.do(lambda: T.transpose(ps_a[1][:, 0:D], agg_n[:, :], ident[:, :]), "turned")
            act.wait("turned")
            act.do(lambda: S.copy(agg_t[:, :], ps_a[1][:, 0:D]), "turned copied")
            pe.wait("turned copied")
            pe.do(lambda: T.matmul(ps_a[1][:, D:2 * D], agg_t[:, :], w_o[:, :], start=True, stop=True),
                  "times Wo")
            dve.wait("times Wo")
            dve.wait_dma(s_gx, 16)
            dve.do(lambda: V.tensor_tensor(y_sum[:, :], ps_a[1][:, D:2 * D], x_blk[:, 0, :], ALU.add), "res")
            dve.wait("res")
            dve.do(lambda: V.tensor_tensor(y_sum[:, :], y_sum[:, :], bias_bc[:, QKV:QKV + D], ALU.add), "y")
            dve.wait("y")
            dve.do(lambda: V.bn_stats(stats[:, :], y_sum[:, :]), "stats")
            dve.wait("stats")
            dve.do(lambda: V.bn_aggr(moments[:, :], stats[:, :]), "moments")
            act.wait("moments")
            act.do(lambda: S.activation(rstd[:, 0:1], moments[:, 1:2], ACT.Ln, bias=eps_c[:, 0:1]), "log")
            act.wait("log")
            act.do(lambda: S.activation(rstd[:, 1:2], rstd[:, 0:1], ACT.Exp, scale=-0.5), "rstd")
            dve.wait("rstd")
            dve.do(lambda: V.tensor_scalar(y_out[:, 0, :], y_sum[:, :], moments[:, 0:1], rstd[:, 1:2],
                                           ALU.subtract, ALU.mult), "normal")
            sp.wait("normal")
            sp.do(lambda: nc.sync.dma_start(y_pad[bass.ds(now["block"] * P, P), :], y_out[:, 0, :])
                  .then_inc(s_gy, 16))
            sp.wait_dma(s_gy, 16)
            dve.wait("normal")
            dve.do(lambda: V.tensor_scalar(g_base, g_base, float(P), None, ALU.add), "next base")
            dve.wait("next base")
            dve.do(lambda: V.nop().then_inc(s_gnode, 1))

        chunk_body()
        ended_body()

        def general_path(engine, name):
            if name == "dve":
                V.memset(g_base, 0.0)
                V.nop().then_inc(s_gnode, 1)
                V.nop().then_inc(s_gfree, 1)
            if name == "sp":
                engine.dma_start(x_pad[0:N, :], x).then_inc(s_gpad, 16)
                if LAST < P:
                    engine.dma_start(x_pad[N:NB * P, :], x_blk[0:P - LAST, 0, :]).then_inc(s_gpad, 16)
                engine.wait_ge(s_gpad, 16 if LAST == P else 32)
            round_ = engine.alloc_register(f"round_{name}")
            engine.reg_mov(round_, 0)
            with engine.Fori(0, NB) as b:
                lo = engine.value_load(lo_row[0:1, bass.ds(b, 1)], min_val=0, max_val=NCH - 1)
                hi = engine.value_load(hi_row[0:1, bass.ds(b + 1, 1)], min_val=1, max_val=NCH)
                if name == "dve":
                    V.memset(g_max, GFAR)
                    V.memset(g_acc, 0.0).then_inc(s_ginit, 1)
                    engine.wait_ge(s_ginit, b + 1)
                    engine.sem_inc(s_passed[name])
                with engine.Fori(lo, hi) as c:
                    now.update(block=b, chunk=c)
                    chunk[name].emit(engine, engine.snap(round_, min_val=0, max_val=NB * NCH),
                                      s_passed[name])
                    engine.reg_add(round_, round_, 1)
                now.update(block=b)
                ended[name].emit(engine, b, s_passed[name])
            if name == "sp":
                engine.dma_start(out, y_pad[0:N, :]).then_inc(s_y[0], 16)
                engine.wait_ge(s_y[0], 16)

        block = ctx.enter_context(nc.Block())

        def program(engine, name, prologue, fast):
            prologue.emit(engine)
            engine.wait_ge(marks["general",][0].semaphore, marks["general",][1])
            general = engine.value_load(general_i[0:1, 0:1], min_val=0, max_val=2 * E)
            with engine.If(general == 0):
                fast.emit(engine)
            with engine.Else():
                general_path(engine, name)

        @block.sync
        def _(engine):
            program(engine, "sp", sp_first, sp)

        @block.gpsimd
        def _(engine):
            program(engine, "pool", pool_first, pool)

        @block.scalar
        def _(engine):
            program(engine, "act", act_first, act)

        @block.vector
        def _(engine):
            program(engine, "dve", dve_first, dve)

        @block.tensor
        def _(engine):
            program(engine, "pe", pe_first, pe)


_INS = ["x", "src", "dst", "L0_gnn_Wq", "L0_gnn_bq", "L0_gnn_Wk", "L0_gnn_bk", "L0_gnn_Wv", "L0_gnn_bv",
        "L0_gnn_We", "L0_gnn_be", "L0_gnn_Wo", "L0_gnn_bo"]


def kernel(**inputs):
    import numpy as _np
    import concourse.bacc as _bacc
    from concourse import mybir as _mybir
    from concourse.bass_utils import run_bass_kernel_spmd as _run

    nc = _bacc.Bacc("TRN2", target_bir_lowering=False, num_devices=1)
    host = {name: _np.ascontiguousarray(inputs[name]) for name in _INS}
    host["x_t"] = _np.ascontiguousarray(_np.asarray(inputs["x"]).T)
    host["edge_t"] = _np.ascontiguousarray(_np.asarray(inputs["edge_attr_64"]).T)
    arrays, args = {}, {}
    for name, a in host.items():
        arrays[f"in_{name}"] = a
        args[name.replace("L0_gnn_", "")] = nc.dram_tensor(
            f"in_{name}", a.shape, _mybir.dt.from_np(a.dtype), kind="ExternalInput").ap()
    out = nc.dram_tensor("out_0", host["x"].shape, _mybir.dt.float32, kind="ExternalOutput").ap()
    graph_attention(nc, out=out, **args)
    r = _run(nc, [arrays], core_ids=[0])
    return r.results[0]["out_0"]
```

```python
from contextlib import ExitStack

import concourse.bass as bass
from concourse import mybir

P = 128
F32 = mybir.dt.float32
I32 = mybir.dt.int32
ALU = mybir.AluOpType
ACT = mybir.ActivationFunctionType
AX = mybir.AxisListType

QUAD = 4
FAR = -3.0e38
LN_EPS = 1e-5
DEN_EPS = 1e-10


class Line:

    def __init__(self, marks, semaphore):
        self.marks, self.semaphore, self.count, self.items = marks, semaphore, 0, []

    def do(self, emit, mark=None):
        if mark is not None:
            mark = mark if isinstance(mark, tuple) else (mark,)
            self.count += 1
            assert mark not in self.marks, mark
            self.marks[mark] = (self, self.count)
        self.items.append(("do", emit, mark))

    def wait(self, *mark):
        self.items.append(("wait", mark, None))

    def wait_dma(self, semaphore, value):
        self.items.append(("dma", semaphore, value))

    def split(self):
        before = Line(self.marks, self.semaphore)
        before.items, self.items = self.items, []
        return before

    def emit(self, engine, round_=None, passed=None):
        for kind, a, b in self.items:
            if kind == "dma":
                if round_ is None:
                    engine.wait_ge(a, b)
                else:
                    engine.wait_ge(a, round_ * b + b)
                    engine.sem_inc(passed)
            elif kind == "wait":
                line, count = self.marks[a]
                if round_ is None:
                    engine.wait_ge(line.semaphore, count)
                else:
                    engine.wait_ge(line.semaphore, round_ * line.count + count)
                    engine.sem_inc(passed)
            else:
                instruction = a()
                if b is not None:
                    instruction.then_inc(self.semaphore, 1)


def graph_attention(nc, x, x_t, src, dst, edge_t, Wq, bq, Wk, bk, Wv, bv, We, be, Wo, bo, out):
    N, D = x.shape
    E = src.shape[0]
    EF, H = We.shape
    HD = D // H
    NB = -(-N // P)
    SLACK = 4 * int((P * E / N) ** 0.5)
    L = -(-(P * E // N + SLACK) // P)
    LM = min(L - 1, -(-(P * E // N) // P))
    C = P * L
    G = -(-L // QUAD)
    assert G >= 8
    STEP = [(g * L // G, (g + 1) * L // G) for g in range(G)]
    LAST_MAIN = LM - STEP[-1][0]
    assert LAST_MAIN > 0
    SCALE = float(HD) ** -0.5
    RP = max(r for r in range(1, P) if E % r == 0)
    RC = E // RP
    GP, NCH = RP, RC
    NE = 2 + L - LM
    NS = NB + 1
    LAST = N - (NB - 1) * P
    KV, QKV = 2 * D, 3 * D
    WV = D + H
    STAGES = 6
    LAG = 5
    EDGE_LAG = 1
    AHEAD = 2

    ctx = ExitStack()
    with ctx:
        def sb(name, shape, dt=F32):
            return ctx.enter_context(nc.sbuf_tensor(name, shape, dt))

        def ps(name, shape):
            return ctx.enter_context(nc.psum_tensor(name, shape, F32))

        def sem(name):
            return ctx.enter_context(nc.semaphore(name))

        kv_table = nc.dram_tensor("kv_table", [N, KV], F32).ap()

        ident = sb("ident", [P, P])
        iota_n = sb("iota_n", [P, P])
        ones = sb("ones", [P, P])
        w_qkv = sb("w_qkv", [P, QKV])
        w_o = sb("w_o", [P, D])
        w_e = sb("w_e", [EF + 1, H])
        bias_bc = sb("bias_bc", [P, QKV + D])
        q_all = sb("q_all", [P, NB, D])
        kv_buf = sb("kv_buf", [P, 2, L, KV])
        onehot = sb("onehot", [P, 2, L, P])
        onehot_t = sb("onehot_t", [P, 2, QUAD * P])
        bias_row = onehot_t[0:1, 0, 0:QKV + D]
        edge_f = [sb(f"edge_f{i}", [EF + 1, C]) for i in range(2)]
        src_i = sb("src_i", [P, 2, L], I32)
        dst_i = sb("dst_i", [P, 2, L], I32)
        dst_f = sb("dst_f", [P, 2, L])
        neg_rel = sb("neg_rel", [P, 2, L])
        distance = sb("distance", [P, 2, QUAD * P])
        prod = sb("prod", [P, 2, QUAD * D])
        score = sb("score", [P, 2, H, L])
        run_fwd = sb("run_fwd", [P, H * L])
        shifted = run_fwd[:, :].rearrange("p (h t) -> p h t", h=H)
        run_max = sb("run_max", [P, H, L])
        end_fwd = sb("end_fwd", [P, H, L])
        end_bwd = sb("end_bwd", [P, H, L])
        not_first = sb("not_first", [P, LM])
        not_last = sb("not_last", [P, LM])
        run_far = sb("run_far", [P, LM])
        cand = sb("cand", [P, 2, H, LM])
        ends = sb("ends", [P, NE, H])
        ends_dst = sb("ends_dst", [P, NE, H])
        seq_val = sb("seq_val", [H, NE * P])
        seq_far = sb("seq_far", [H, NE * P + 1])
        seq_f = sb("seq_f", [H, NE * P])
        seq_dst = seq_f
        seq_b = sb("seq_b", [H, NE * P])
        weight = sb("weight", [P, 2, H, L])
        wv = sb("wv", [P, 2, QUAD, WV])
        den = sb("den", [P, H])
        rec = sb("rec", [P, H])
        agg_n = sb("agg_n", [P, D])
        y_sum = sb("y_sum", [P, D])
        agg_t = sb("agg_t", [P, D])
        x_blk = sb("x_blk", [P, 2, D])
        stats = sb("stats", [P, 6])
        moments = sb("moments", [P, 2])
        rstd = sb("rstd", [P, 2])
        eps_c = sb("eps_c", [P, 1])
        y_out = sb("y_out", [P, 2, D])
        xt = onehot[:, :, :, :].rearrange("p a l n -> p (a l n)")[:, 0:N]
        kv_stage = kv_buf[:, 0, 0:2 * STAGES, :].rearrange("p (s a) d -> p s a d", a=2)
        def in_kv(parts, half, slot, n, at=0):
            return kv_buf[0:parts, half, slot:slot + -(-n // KV), :].rearrange("p a b -> p (a b)")[:, at:at + n]

        ROW_SLOTS = -(-RC // KV)
        dst2d_i = in_kv(RP, 0, 2 * STAGES, RC).bitcast(I32)
        row_f = in_kv(NS, 0, 2 * STAGES + ROW_SLOTS, RC)
        row_i = row_f.bitcast(I32)
        sort_f = in_kv(RP, 1, 0, RC - 1)
        assert 2 * STAGES + 2 * ROW_SLOTS <= LM and 2 * L * P >= N
        assert L > 15 and 2 * P <= KV and H * P <= 4 * KV
        g_kv = in_kv(GP, 1, 0, KV)
        g_spread = in_kv(GP, 1, 1, H * P)
        g_z = in_kv(P, 1, 5, H * GP)
        g_wv = in_kv(GP, 1, 9, WV)
        g_acc = in_kv(P, 1, 10, WV)
        g_hot = in_kv(GP, 1, 11, P)
        g_hot_t = in_kv(P, 1, 12, GP)
        g_mask = in_kv(P, 1, 12, GP, P)
        g_prod = in_kv(GP, 1, 13, D)
        g_score, g_in, g_far, g_dst_f, g_shift, g_shift2 = (
            in_kv(GP, 1, 14, n, at) for n, at in ((H, 0), (1, 8), (1, 9), (1, 10), (H, 16), (H, 24)))
        g_base, g_max, g_new, g_zmax, g_drop, g_keep = (
            in_kv(P, 1, 14, n, at) for n, at in ((1, 64), (H, 72), (H, 80), (H, 88), (H, 96), (H, 104)))
        g_src, g_dst = (in_kv(GP, 1, 15, 1, at).bitcast(I32) for at in (0, 1))
        g_edge = edge_f[0][:, 0:GP]
        idle = cand[:, :, :, :].rearrange("p k h t -> p (k h t)")
        iota_i = idle[:, 0:P].bitcast(I32)
        border_i = idle[:, P:P + NS].bitcast(I32)
        border = idle[:, P + NS:P + 2 * NS]
        below = idle[:, P + 2 * NS:P + 3 * NS]
        border_p = sb("border_p", [P, 1])
        border_pi = sb("border_pi", [P, 1], I32)
        last_f = sb("last_f", [P, 1])
        rows_f = sb("rows_f", [P, 1])
        rows_i = sb("rows_i", [P, 1], I32)
        cnt = sb("cnt", [P, 1])
        start_f = sb("start_f", [P, 1])
        first_f = sb("first_f", [P, 1])
        falls = sb("falls", [P, 1])
        row_s = prod[0:1, 0, 0:3 * P]
        row_x = prod[0:1, 1, 0:2 * P]
        row_b = prod[0:1, 1, 2 * P:2 * P + NS]
        sorted_f = sb("sorted_f", [1, 8])
        lo_row = sb("lo_row", [1, NS], I32)
        hi_row = sb("hi_row", [1, NS], I32)
        tail_row = sb("tail_row", [1, NB], I32)
        landed_row = sb("landed_row", [1, NB], I32)
        step_tiles = prod[0:1, 1, 3 * P:3 * P + NB]
        total_tiles = prod[0:1, 0, 3 * P:3 * P + NB]
        general_i = sb("general_i", [1, 1], I32)
        start_row = sb("start_row", [1, NS], I32)

        ps_t = [ps(f"ps_t{i}", [P, 512]) for i in range(2)]
        ps_q = [ps(f"ps_q{i}", [P, 512]) for i in range(2)]
        ps_e = ps("ps_e", [P, 512])
        ps_a = [ps(f"ps_a{i}", [P, 512]) for i in range(2)]
        ps_s = ps("ps_s", [P, 512])

        back_max = ps_s[:, 0:NE * H]
        assert L * H <= 512 and NE * P <= 512

        def sums(b):
            return ps_a[b % 2][:, 0:WV]

        def turned(b):
            return ps_a[b % 2][:, WV:WV + D]

        def projected(b):
            return ps_a[b % 2][:, WV + D:WV + 2 * D]

        s_wkv, s_bias, s_wrest = sem("s_wkv"), sem("s_bias"), sem("s_wrest")
        s_xt = [sem(f"s_xt{i}") for i in range(min(7, NB))]
        s_dst2d = sem("s_dst2d")
        s_rows = sem("s_rows")
        s_table = [sem(f"s_table{i}") for i in range(STAGES)]
        s_src = [sem(f"s_src{i}") for i in range(2)]
        s_dst = [sem(f"s_dst{i}") for i in range(2)]
        s_edge = [sem(f"s_edge{i}") for i in range(2)]
        s_x = [sem(f"s_x{i}") for i in range(2)]
        s_kv = [[sem(f"s_kv{i}_{g}") for g in range(G)] for i in range(2)]
        s_y = [sem(f"s_y{i}") for i in range(2)]
        marks = {}
        pool, act, dve, pe = (Line(marks, sem(f"s_{n}")) for n in ("pool", "act", "dve", "pe"))
        sp = Line(marks, None)
        V, T, S = nc.vector, nc.tensor, nc.scalar

        INDEX_LOADS = 16 * (1 + L - LM)

        def kv_ready(b, g):
            return s_kv[b % 2][g], 16 * (STEP[g][1] - STEP[g][0]) * (b // 2 + 1)

        def rows(b):
            return P if b < NB - 1 else LAST

        for i, v, s in ((1, bk, s_bias), (2, bv, s_bias), (0, bq, s_wrest), (3, bo, s_wrest)):
            act.do(lambda i=i, v=v, s=s: nc.scalar.dma_start(
                bias_row[:, i * D:(i + 1) * D], v.rearrange("(a d) -> a d", a=1)).then_inc(s, 16))
        pool.do(lambda: nc.gpsimd.memset(ident[:, :], 0.0), "ident zero")
        pool.do(lambda: nc.gpsimd.iota(iota_i[:, :], [[1, P]], base=0, channel_multiplier=0))
        pool.do(lambda: nc.gpsimd.iota(border_i[:, :], [[P, NS]], base=0, channel_multiplier=0))
        pool.do(lambda: nc.gpsimd.iota(border_pi[:, :], [[0, 1]], base=0, channel_multiplier=P), "iotas")
        pool.wait("ident zero")
        pool.do(lambda: nc.gpsimd.affine_select(
            out=ident[:, :], in_=ident[:, :], compare_op=ALU.not_equal, fill=1.0, base=0,
            pattern=[[-1, P]], channel_multiplier=1), "ident")

        pool.wait("ident")
        for i in range(2):
            pool.do(lambda i=i: nc.gpsimd.memset(kv_buf[:, i, LM:L, :], 0.0), ("tail zero", i))
        pool.wait("tail zero", 1)
        for i in range(2):
            pool.do(lambda i=i: nc.gpsimd.memset(edge_f[i][EF:EF + 1, :], 1.0), ("edge ones", i))

        dve.do(lambda: V.memset(ones[:, :], 1.0), "ones")
        dve.do(lambda: V.memset(eps_c[:, :], LN_EPS))
        dve.do(lambda: V.memset(x_blk[:, :, :], 0.0), "x zero")
        dve.wait("iotas")
        dve.do(lambda: V.tensor_copy(iota_n[:, :], iota_i[:, :]), "iota_n")
        dve.do(lambda: V.tensor_copy(border[:, :], border_i[:, :]))
        dve.do(lambda: V.tensor_copy(border_p[:, :], border_pi[:, :]))

        def spread_bias(i, n):
            span = slice(i * D, (i + n) * D)
            pe.do(lambda: T.matmul(ps_e[:, span], ones[0:1, :], bias_row[:, span], start=True, stop=True),
                  ("bias spread", i))
            dve.wait("bias spread", i)
            dve.do(lambda: V.tensor_copy(bias_bc[:, span], ps_e[:, span]), ("bias", i))

        pe.wait("ones")
        pe.wait_dma(s_bias, 32)
        spread_bias(1, 2)

        banks = (ps_q[0], ps_q[1], ps_t[0], ps_t[1])

        def in_groups(n):
            return [(b, min(n, NB - 1 - b)) for b in range(0, NB - 1, n)] + [(NB - 1, 1)]

        def bias_of(lo, hi, n, count):
            return bias_bc[0:n, lo:hi].rearrange("p (a d) -> p a d", a=1).to_broadcast([n, count, hi - lo])

        KV_GROUPS = in_groups(2)
        Q_GROUPS = in_groups(4)
        TABLE_DONE = [16 * len(range(i, len(KV_GROUPS), STAGES)) for i in range(STAGES)]
        xt_blocks = -(-NB // len(s_xt))

        pe.wait_dma(s_wkv, 32)
        dve.wait("bias", 1)

        def project_kv(j):
            b, count = KV_GROUPS[j]
            n, bank = rows(b), banks[j % 4]
            if j >= 4:
                pe.wait("staged", j - 4)
            for k in range(b, b + count):
                if k % xt_blocks == 0:
                    pe.wait_dma(s_xt[k // xt_blocks], 16)
                pe.do(lambda k=k: T.matmul(bank[0:n, (k - b) * KV:(k - b + 1) * KV],
                                           xt[:, k * P:k * P + n], w_qkv[:, D:QKV],
                                           start=True, stop=True),
                      ("projected kv", j) if k == b + count - 1 else None)
            dve.wait("projected kv", j)
            if j >= STAGES:
                dve.wait_dma(s_table[j % STAGES], 16 * (j // STAGES))
            dve.do(lambda: V.tensor_tensor(
                kv_stage[0:n, j % STAGES, 0:count, :],
                bank[0:n, 0:count * KV].rearrange("p (a d) -> p a d", a=count),
                bias_of(D, QKV, n, count), ALU.add), ("staged", j))

        def project_q(j):
            b, count = Q_GROUPS[j]
            n, bank = rows(b), banks[j % 4]
            if j < 4:
                pe.wait("staged", len(KV_GROUPS) - 1)
            else:
                pe.wait("q", j - 4)
            for k in range(b, b + count):
                pe.do(lambda k=k: T.matmul(bank[0:n, (k - b) * D:(k - b + 1) * D],
                                           xt[:, k * P:k * P + n], w_qkv[:, 0:D], start=True, stop=True),
                      ("projected q", j) if k == b + count - 1 else None)
            dve.wait("projected q", j)
            dve.do(lambda: V.tensor_tensor(
                q_all[0:n, b:b + count, :],
                bank[0:n, 0:count * D].rearrange("p (a d) -> p a d", a=count),
                bias_of(0, D, n, count), ALU.add), ("q", j))

        def find_windows():
            dve.wait_dma(s_dst2d, 16)
            dve.do(lambda: V.tensor_copy(last_f[0:RP, :], dst2d_i[:, RC - 1:RC]), "row last")
            dve.do(lambda: V.tensor_copy(first_f[0:RP, :], dst2d_i[:, 0:1]))
            dve.wait("row last")
            dve.do(lambda: V.tensor_scalar(below[0:RP, :], border[0:RP, :], last_f[0:RP, 0:1], None,
                                           ALU.is_gt), "rows below")
            yield
            pe.wait("rows below")
            pe.do(lambda: T.matmul(ps_s[0:NS, 0:1], below[0:RP, :], ones[0:RP, 0:1],
                                   start=True, stop=True), "rows counted")
            dve.wait("rows counted")
            dve.do(lambda: V.tensor_scalar(rows_f[0:NS, :], ps_s[0:NS, 0:1], float(RP - 1), None,
                                           ALU.min), "border row")
            dve.wait("border row")
            dve.do(lambda: V.tensor_copy(rows_i[0:NS, :], rows_f[0:NS, :]), "border row int")
            pool.wait("border row int")
            pool.do(lambda: nc.gpsimd.indirect_dma_start(
                row_i, None, dst.rearrange("(r c) -> r c", c=RC),
                bass.IndirectOffsetOnAxis(ap=rows_i[0:NS, 0:1], axis=0)).then_inc(s_rows, 16))
            yield
            dve.do(lambda: V.tensor_tensor(sort_f, dst2d_i[:, 1:RC], dst2d_i[:, 0:RC - 1], ALU.is_lt), "falls")
            dve.wait("falls")
            yield
            dve.do(lambda: V.tensor_reduce(falls[0:RP, :], sort_f, AX.X, ALU.add), "falls by row")
            yield
            dve.wait_dma(s_rows, 16)
            dve.do(lambda: V.tensor_scalar(row_f, row_i, border_p[0:NS, 0:1], None, ALU.is_lt), "row below")
            dve.wait("row below")
            yield
            dve.do(lambda: V.tensor_reduce(cnt[0:NS, :], row_f, AX.X, ALU.add), "row count")
            dve.wait("row count")
            dve.do(lambda: V.scalar_tensor_tensor(
                out=start_f[0:NS, 0:1], in0=rows_f[0:NS, :], scalar=float(RC), in1=cnt[0:NS, :],
                op0=ALU.mult, op1=ALU.add), "border edge")
            yield
            yield
            pe.wait("border edge")
            pe.wait("ident")
            pe.do(lambda: T.transpose(ps_s[0:1, 0:NS], start_f[0:NS, 0:1], ident[0:NS, 0:NS]))
            pe.do(lambda: T.matmul(ps_s[0:1, NS:NS + 1], falls[0:RP, :], ones[0:RP, 0:1], start=True,
                                   stop=True))
            pe.do(lambda: T.transpose(ps_s[0:1, P:P + RP], first_f[0:RP, :], ident[0:RP, 0:RP]))
            pe.do(lambda: T.transpose(ps_s[0:1, 2 * P:2 * P + RP], last_f[0:RP, :], ident[0:RP, 0:RP]),
                  "rows turned")
            yield
            dve.wait("rows turned")
            dve.do(lambda: V.tensor_copy(row_s[:, 0:NS + 1], ps_s[0:1, 0:NS + 1]))
            dve.do(lambda: V.tensor_copy(row_s[:, P:P + RP], ps_s[0:1, P:P + RP]))
            dve.do(lambda: V.tensor_copy(row_s[:, 2 * P:2 * P + RP], ps_s[0:1, 2 * P:2 * P + RP]), "row s")
            dve.wait("row s")
            borders = row_s[:, 0:NS]
            dve.do(lambda: V.tensor_tensor(row_x[:, 0:RP - 1], row_s[:, P + 1:P + RP],
                                           row_s[:, 2 * P:2 * P + RP - 1], ALU.is_lt), "row falls")
            dve.do(lambda: V.tensor_scalar(row_b[:, :], borders, float(E - C), None, ALU.min), "start")
            dve.wait("row falls")
            dve.do(lambda: V.tensor_reduce(sorted_f[:, 0:1], row_x[:, 0:RP - 1], AX.X, ALU.add), "x falls")
            dve.wait("start")
            dve.do(lambda: V.tensor_copy(start_row[:, :], row_b[:, :]), "starts")
            dve.do(lambda: V.tensor_tensor(row_x[:, P:P + NB], row_s[:, 1:NS], row_b[:, 0:NB], ALU.subtract),
                   "needed")
            dve.wait("needed")
            needed = row_x[:, P:P + NB]
            dve.do(lambda: V.tensor_scalar(tail_row[:, :], needed, float(P * LM), 0.0, ALU.subtract, ALU.max))
            dve.do(lambda: V.tensor_scalar(step_tiles, needed, float(P * LM), float(LAST_MAIN), ALU.is_gt,
                                           ALU.add), ("tiles", LM))
            for t in range(LM + 1, L):
                dve.wait("tiles", t - 1)
                dve.do(lambda t=t: V.scalar_tensor_tensor(
                    out=step_tiles, in0=needed, scalar=float(P * t), in1=step_tiles, op0=ALU.is_gt,
                    op1=ALU.add), ("tiles", t))
            dve.wait("tiles", L - 1)
            for i in range(min(2, NB)):
                dve.do(lambda i=i: V.tensor_tensor_scan(
                    total_tiles[:, i::2], ones[0:1, i:NB:2], step_tiles[:, i::2], 0.0, ALU.mult, ALU.add),
                    ("total tiles", i))
                dve.wait("total tiles", i)
            dve.do(lambda: V.tensor_scalar(landed_row[:, :], total_tiles, 16.0, None, ALU.mult))
            dve.do(lambda: V.tensor_scalar(row_x[:, P:P + NB], row_x[:, P:P + NB], float(C), None,
                                           ALU.is_gt), "over")
            dve.wait("over")
            yield
            dve.do(lambda: V.tensor_reduce(sorted_f[:, 1:2], row_x[:, P:P + NB], AX.X, ALU.add))
            dve.wait("x falls")
            dve.do(lambda: V.tensor_tensor(sorted_f[:, 2:3], sorted_f[:, 0:1], row_s[:, NS:NS + 1], ALU.add),
                   "unsorted")
            dve.wait("unsorted")
            dve.do(lambda: V.tensor_tensor(sorted_f[:, 3:4], sorted_f[:, 1:2], sorted_f[:, 2:3], ALU.add),
                   "general f")
            dve.do(lambda: V.tensor_scalar(sorted_f[:, 4:5], sorted_f[:, 2:3], 1.0, 4.0 * NCH, ALU.min,
                                           ALU.mult), "everything")
            yield
            dve.do(lambda: V.tensor_scalar(row_x[:, 0:NS], borders, 1.0 / GP, None, ALU.mult), "chunk f")
            dve.wait("chunk f")
            dve.do(lambda: V.tensor_scalar(row_b[:, :], row_x[:, 0:NS], -1.0, sorted_f[:, 4:5], ALU.add,
                                           ALU.subtract), "lo f")
            dve.wait("lo f")
            dve.do(lambda: V.tensor_scalar(lo_row[:, :], row_b[:, :], 0.0, None, ALU.max), "lo")
            dve.wait("lo")
            dve.do(lambda: V.tensor_scalar(row_b[:, :], row_x[:, 0:NS], 1.0, sorted_f[:, 4:5], ALU.add,
                                           ALU.add), "hi f")
            dve.wait("hi f")
            dve.do(lambda: V.tensor_scalar(hi_row[:, :], row_b[:, :], float(NCH), None, ALU.min), "hi")
            dve.do(lambda: V.tensor_copy(general_i[:, :], sorted_f[:, 3:4]), "general")

        windows = find_windows()
        for j in range(len(KV_GROUPS)):
            project_kv(j)
            if j % 2:
                next(windows, None)
        for _ in windows:
            pass
        for j, (b, count) in enumerate(KV_GROUPS):
            act.wait("staged", j)
            act.do(lambda j=j, b=b, count=count: nc.scalar.dma_start(
                kv_table[b * P:b * P + (count - 1) * P + rows(b), :]
                .rearrange("(a p) d -> p a d", a=count),
                kv_stage[0:rows(b), j % STAGES, 0:count, :])
                .then_inc(s_table[j % STAGES], 16))
        dve.do(lambda: V.memset(q_all[:, NB - 1, :], 0.0), "q zero")
        pe.wait_dma(s_wrest, 96)
        spread_bias(0, 1)
        pe.wait("bias", 0)
        spread_bias(3, 1)
        dve.wait_dma(s_wrest, 96)
        dve.wait("bias", 0)
        dve.do(lambda: V.tensor_scalar(w_qkv[:, 0:D], w_qkv[:, 0:D], SCALE, None, ALU.mult))
        dve.do(lambda: V.tensor_scalar(bias_bc[:, 0:D], bias_bc[:, 0:D], SCALE, None, ALU.mult), "scaled")
        dve.wait("scaled")
        dve.wait("q zero")
        pe.wait("scaled")
        for j in range(len(Q_GROUPS)):
            project_q(j)
        for line in (pe, act):
            line.wait("q", len(Q_GROUPS) - 1)

        for i in range(STAGES):
            pool.wait_dma(s_table[i], TABLE_DONE[i])

        pe.wait("edge ones", 1)
        act.wait("x zero")
        pool_first, act_first, dve_first, pe_first = (
            line.split() for line in (pool, act, dve, pe))
        def gather(b, t, g):
            nc.gpsimd.indirect_dma_start(
                kv_buf[:, b % 2, t, :], None, kv_table,
                bass.IndirectOffsetOnAxis(ap=src_i[:, b % 2, t:t + 1], axis=0)).then_inc(s_kv[b % 2][g], 16)

        tail = [None]

        def gather_tail(b, t, g):
            if t == LM:
                tail[0] = nc.gpsimd.value_load(tail_row[0:1, b:b + 1], min_val=0, max_val=E)
            with nc.gpsimd.If(tail[0] > P * (t - LM)):
                gather(b, t, g)

        for b in range(NB):
            pool.wait_dma(s_src[b % 2], INDEX_LOADS * (b // 2 + 1))
            for g, (t0, t1) in enumerate(STEP):
                if b >= 2:
                    pool.wait("weighted", (b - 2) * G + g)
                for t in range(t0, t1):
                    if t < LM:
                        pool.do(lambda b=b, t=t, g=g: gather(b, t, g))
                    else:
                        pool.do(lambda b=b, t=t, g=g: gather_tail(b, t, g))

        def indices(b):
            i = b % 2
            dve.wait_dma(s_dst[i], INDEX_LOADS * (b // 2 + 1))
            dve.do(lambda: V.tensor_copy(dst_f[:, i, :], dst_i[:, i, :]), ("dst", b))
            dve.wait("dst", b)
            if b >= 2:
                dve.wait("onehot", (b - 1) * G - 1)
            dve.do(lambda: V.tensor_scalar(neg_rel[:, i, :], dst_f[:, i, :], -1.0, float(P * b),
                                           ALU.mult, ALU.add), ("dst rel", b))

        def wait_last_step(b):
            landed = V.value_load(landed_row[0:1, b:b + 1], min_val=16, max_val=16 * NB * QUAD)
            V.wait_ge(s_kv[b % 2][G - 1], landed)
            V.sem_inc(s_passed["dve"])

        def multiply(q):
            b, (t0, t1) = q // G, STEP[q % G]
            n = t1 - t0
            dve.wait("q by edge", q)
            if q % G < G - 1:
                dve.wait_dma(*kv_ready(b, q % G))
            else:
                dve.do(lambda b=b: wait_last_step(b))
            if q >= 2:
                dve.wait("dot", q - 2)
            dve.do(lambda: V.tensor_tensor(
                prod[:, q % 2, 0:n * D].rearrange("p (t d) -> p t d", d=D),
                ps_q[q % 2][:, 0:n * D].rearrange("p (t d) -> p t d", d=D),
                kv_buf[:, b % 2, t0:t1, 0:D], ALU.mult), ("product", q))

        def dot(q):
            b, (t0, t1) = q // G, STEP[q % G]
            dve.wait("product", q)
            dve.do(lambda: V.tensor_reduce(
                score[:, b % 2, :, t0:t1].rearrange("p h t -> p t h"),
                prod[:, q % 2, 0:(t1 - t0) * D].rearrange("p (t h d) -> p t h d", h=H, d=HD),
                AX.X, ALU.add), ("dot", q))

        def weigh(q):
            b, (t0, t1) = q // G, STEP[q % G]
            dve.wait("weights", b)
            if q >= 2:
                dve.wait("summed", q - 2)
            dve.do(lambda: V.tensor_tensor(
                wv[:, q % 2, 0:t1 - t0, 0:D].rearrange("p t (h d) -> p t h d", d=HD),
                kv_buf[:, b % 2, t0:t1, D:KV].rearrange("p t (h d) -> p t h d", d=HD),
                weight[:, b % 2, :, t0:t1].rearrange("p h (t a) -> p t h a", a=1)
                .to_broadcast([P, t1 - t0, H, HD]), ALU.mult), ("weighted", q))

        def flat(a):
            return a.rearrange("p h t -> p (h t)")

        def per_edge(a, n):
            return a.rearrange("p (a t) -> p a t", a=1).to_broadcast([P, H, n])

        def by_end(a):
            return a[:, 0:2 * P].rearrange("h (p e) -> h e p", e=2)

        def sequence(to, mark):
            dve.do(lambda: V.tensor_copy(by_end(to), ps_s[0:H, 0:2 * P].rearrange("h (e p) -> h e p", e=2)))
            dve.do(lambda: V.tensor_copy(to[:, 2 * P:NE * P], ps_s[0:H, 2 * P:NE * P]), mark)

        def runs_of_dst(b):
            d = dst_f[:, b % 2, :]
            dve.do(lambda: V.memset(end_fwd[:, :, 0:1], FAR))
            dve.do(lambda: V.memset(end_fwd[:, :, LM:L], FAR))
            dve.do(lambda: V.memset(end_bwd[:, :, LM - 1:L], FAR))
            dve.do(lambda: V.tensor_tensor(run_far[:, 1:LM], d[:, 1:LM], d[:, 0:LM - 1], ALU.not_equal),
                   ("changes", b))
            dve.wait("changes", b)
            dve.do(lambda: V.tensor_scalar(end_fwd[:, :, 1:LM], per_edge(run_far[:, 1:LM], LM - 1), FAR,
                                           None, ALU.mult))
            dve.do(lambda: V.tensor_scalar(end_bwd[:, :, 0:LM - 1], per_edge(run_far[:, 1:LM], LM - 1),
                                           FAR, None, ALU.mult), ("run ends", b))
            for away, end in ((not_first, 0), (not_last, LM - 1)):
                dve.do(lambda away=away, end=end: V.tensor_scalar(
                    away[:, :], d[:, 0:LM], d[:, end:end + 1], FAR, ALU.not_equal, ALU.mult),
                    ("away", b) if end else None)

        def run_maxima(b):
            s = score[:, b % 2, :, :]
            dve.wait("edge terms", b)
            dve.wait("dot", (b + 1) * G - 1)
            dve.do(lambda: V.tensor_tensor(s, s, ps_e[:, 0:L * H].rearrange("p (t h) -> p h t", h=H),
                                           ALU.add), ("score", b))
            dve.wait("score", b)
            dve.wait("run ends", b)
            if b >= 1:
                dve.wait("weights", b - 1)
            dve.do(lambda: V.tensor_tensor_scan(run_fwd[:, :], flat(end_fwd[:, :, :]), flat(s), FAR,
                                                ALU.add, ALU.max), ("forward", b))
            dve.wait("forward", b)
            dve.do(lambda: V.tensor_tensor_scan(
                flat(run_max[:, :, :])[:, ::-1], flat(end_bwd[:, :, :])[:, ::-1], run_fwd[:, ::-1],
                FAR, ALU.add, ALU.max), ("backward", b))
            dve.wait("backward", b)
            dve.do(lambda: V.tensor_copy(ends[:, 0, :], run_max[:, :, 0]))
            dve.do(lambda: V.tensor_copy(ends[:, 1:NE, :], run_max[:, :, LM - 1:L].rearrange("p h e -> p e h")),
                   ("ends", b))

        def dst_of_ends(b):
            d = dst_f[:, b % 2, :]
            if b >= 1:
                dve.wait("ends dst turned", b - 1)
            dve.do(lambda: V.tensor_copy(ends_dst[:, 0, :], d[:, 0:1].to_broadcast([P, H])))
            dve.do(lambda: V.tensor_copy(
                ends_dst[:, 1:NE, :],
                d[:, LM - 1:L].rearrange("p (e a) -> p e a", a=1).to_broadcast([P, NE - 1, H])),
                ("ends dst", b))

        def turn_dst(b):
            pe.wait("ends dst", b)
            if b >= 1:
                pe.wait("tail maxima", b - 1)
            for k in range(NE):
                pe.do(lambda k=k: T.transpose(ps_s[0:H, k * P:(k + 1) * P], ends_dst[:, k, :], ident[:, :]),
                      ("ends dst turned", b) if k == NE - 1 else None)

        def sequence_ends(b):
            dve.wait("ends dst turned", b)
            sequence(seq_dst, ("sequence dst", b))
            dve.wait("sequence dst", b)
            dve.do(lambda: V.memset(seq_far[:, ::NE * P], FAR))
            dve.do(lambda: V.tensor_tensor(seq_far[:, 1:NE * P], seq_dst[:, 1:NE * P],
                                           seq_dst[:, 0:NE * P - 1], ALU.not_equal), ("seq changes", b))
            dve.wait("seq changes", b)
            dve.do(lambda: V.tensor_scalar(seq_far[:, 1:NE * P], seq_far[:, 1:NE * P], FAR, None, ALU.mult),
                   ("seq ends", b))

        def turn_ends(b):
            pe.wait("ends", b)
            pe.wait("sequence dst", b)
            for k in range(NE):
                pe.do(lambda k=k: T.transpose(ps_s[0:H, k * P:(k + 1) * P], ends[:, k, :], ident[:, :]),
                      ("ends turned", b) if k == NE - 1 else None)

        def crossing_maxima(b):
            dve.wait("ends turned", b)
            sequence(seq_val, ("sequence", b))
            dve.wait("sequence", b)
            dve.wait("seq ends", b)
            dve.do(lambda: V.tensor_tensor_scan(seq_f[:, :], seq_far[:, 0:NE * P], seq_val[:, :], FAR,
                                                ALU.add, ALU.max), ("seq forward", b))
            dve.wait("seq forward", b)
            dve.do(lambda: V.tensor_tensor_scan(
                seq_b[:, ::-1], seq_far[:, 1:NE * P + 1][:, ::-1], seq_f[:, ::-1], FAR, ALU.add, ALU.max),
                ("seq backward", b))

        def turn_crossing(b):
            pe.wait("seq backward", b)
            for k in range(NE):
                part = by_end(seq_b)[:, k, :] if k < 2 else seq_b[:, k * P:(k + 1) * P]
                pe.do(lambda k=k, part=part: T.transpose(
                    back_max[:, k * H:(k + 1) * H], part, ident[0:H, 0:H]),
                    ("crossing", b) if k == NE - 1 else None)

        def edge_maxima(b):
            s = score[:, b % 2, :, :]
            dve.wait("crossing", b)
            for k, away in enumerate((not_first, not_last)):
                dve.do(lambda k=k, away=away: V.tensor_tensor(
                    cand[:, k, :, :],
                    back_max[:, k * H:(k + 1) * H].rearrange("p (h a) -> p h a", a=1)
                    .to_broadcast([P, H, LM]),
                    per_edge(away[:, :], LM), ALU.add), ("candidates", b) if k == 1 else None)
            dve.do(lambda: V.tensor_copy(run_max[:, :, LM:L],
                                         back_max[:, 2 * H:NE * H].rearrange("p (e h) -> p h e", h=H)),
                   ("tail maxima", b))
            dve.wait("candidates", b)
            dve.do(lambda: V.tensor_tensor(cand[:, 0, :, :], cand[:, 0, :, :], cand[:, 1, :, :], ALU.max),
                   ("larger", b))
            dve.wait("larger", b)
            dve.do(lambda: V.tensor_tensor(run_max[:, :, 0:LM], run_max[:, :, 0:LM], cand[:, 0, :, :],
                                           ALU.max), ("maximum", b))
            dve.wait("maximum", b)
            dve.do(lambda: V.tensor_tensor(shifted[:, :, :], s, run_max[:, :, :], ALU.subtract),
                   ("shifted", b))

        def divide(b):
            dve.wait("summed", (b + 1) * G - 1)
            dve.do(lambda: V.tensor_scalar(den[:, :], sums(b)[:, D:WV], DEN_EPS, None, ALU.add), ("den", b))
            dve.wait("den", b)
            dve.do(lambda: V.reciprocal(rec[:, :], den[:, :]), ("rec", b))
            dve.wait("rec", b)
            if b >= 1:
                dve.wait("aggregate turned", b - 1)
            dve.do(lambda: V.tensor_tensor(
                agg_n[:, :].rearrange("p (h d) -> p h d", d=HD),
                sums(b)[:, 0:D].rearrange("p (h d) -> p h d", d=HD),
                rec[:, :].rearrange("p (h a) -> p h a", a=1).to_broadcast([P, H, HD]), ALU.mult),
                ("aggregate", b))

        def residual(b):
            dve.wait("times Wo", b)
            dve.wait_dma(s_x[b % 2], 16 * (b // 2 + 1))
            dve.do(lambda: V.tensor_tensor(y_sum[:, :], projected(b), x_blk[:, b % 2, :], ALU.add),
                   ("residual", b))
            dve.wait("residual", b)
            dve.do(lambda: V.tensor_tensor(y_sum[:, :], y_sum[:, :], bias_bc[:, QKV:QKV + D], ALU.add),
                   ("y", b))
            dve.wait("y", b)
            dve.do(lambda: V.bn_stats(stats[:, :], y_sum[:, :]), ("stats", b))
            dve.wait("stats", b)
            dve.do(lambda: V.bn_aggr(moments[:, :], stats[:, :]), ("moments", b))

        def normalise(b):
            dve.wait("rstd", b)
            if b >= 2:
                dve.wait_dma(s_y[b % 2], 16 * (b // 2))
            dve.do(lambda: V.tensor_scalar(y_out[:, b % 2, :], y_sum[:, :], moments[:, 0:1], rstd[:, 1:2],
                                           ALU.subtract, ALU.mult), ("normal", b))

        def turn_onehot(q):
            b, (t0, t1) = q // G, STEP[q % G]
            pe.wait("onehot", q)
            if q >= 2:
                pe.wait("onehot copied", q - 2)
            for t in range(t0, t1):
                pe.do(lambda t=t: T.transpose(ps_t[q % 2][:, (t - t0) * P:(t - t0 + 1) * P],
                                              onehot[:, b % 2, t, :], ident[:, :]),
                      ("onehot turned", q) if t == t1 - 1 else None)

        def spread_q(q):
            b, (t0, t1) = q // G, STEP[q % G]
            pe.wait("onehot copied", q)
            if q >= 2:
                pe.wait("product", q - 2)
            for t in range(t0, t1):
                pe.do(lambda t=t: T.matmul(
                    ps_q[q % 2][:, (t - t0) * D:(t - t0 + 1) * D],
                    onehot_t[:, q % 2, (t - t0) * P:(t - t0 + 1) * P], q_all[:, b, :],
                    start=True, stop=True), ("q by edge", q) if t == t1 - 1 else None)

        def edge_terms(q):
            b, g = divmod(q, G)
            if g < EDGE_LAG:
                return
            if g == EDGE_LAG:
                pe.wait_dma(s_edge[b % 2], 16 * (b // 2 + 1))
                if b >= 1:
                    pe.wait("score", b - 1)
            for t in range((g - EDGE_LAG) * L // (G - EDGE_LAG), (g - EDGE_LAG + 1) * L // (G - EDGE_LAG)):
                span = slice(t, P * LM, LM) if t < LM else slice(P * t, P * (t + 1))
                pe.do(lambda t=t, span=span: T.matmul(ps_e[:, t * H:(t + 1) * H], edge_f[b % 2][:, span],
                                                      w_e[:, :], start=True, stop=True),
                      ("edge terms", b) if t == L - 1 else None)

        def sum_step(q):
            b, (t0, t1) = q // G, STEP[q % G]
            pe.wait("weighted", q)
            pe.wait("weights beside", q)
            if t0 == 0 and b >= 2:
                pe.wait("residual", b - 2)
            for t in range(t0, t1):
                pe.do(lambda t=t: T.matmul(sums(b), onehot[:, b % 2, t, :], wv[:, q % 2, t - t0, :],
                                           start=(t == 0), stop=(t == L - 1)),
                      ("summed", q) if t == t1 - 1 else None)

        def turn_aggregate(b):
            pe.wait("aggregate", b)
            pe.do(lambda: T.transpose(turned(b), agg_n[:, :], ident[:, :]), ("aggregate turned", b))

        def times_wo(b):
            pe.wait("turned copied", b)
            pe.do(lambda: T.matmul(projected(b), agg_t[:, :], w_o[:, :], start=True, stop=True),
                  ("times Wo", b))

        def build_onehot(q):
            b, (t0, t1) = q // G, STEP[q % G]
            act.wait("dst rel", b)
            if q >= 2:
                act.wait("onehot", q - 2)
            for t in range(t0, t1):
                act.do(lambda t=t: S.activation(distance[:, q % 2, (t - t0) * P:(t - t0 + 1) * P], iota_n[:, :],
                                                ACT.Abs, bias=neg_rel[:, b % 2, t:t + 1]),
                       ("distance", q) if t == t1 - 1 else None)
            act.wait("distance", q)
            if b >= 2:
                act.wait("summed", q - 2 * G)
            act.do(lambda: S.activation(
                onehot[:, b % 2, t0:t1, :].rearrange("p t n -> p (t n)"),
                distance[:, q % 2, 0:(t1 - t0) * P], ACT.Relu, bias=1.0, scale=-1.0), ("onehot", q))

        def copy_onehot(q):
            n = (STEP[q % G][1] - STEP[q % G][0]) * P
            act.wait("onehot turned", q)
            if q >= 2:
                act.wait("q by edge", q - 2)
            act.do(lambda: S.copy(onehot_t[:, q % 2, 0:n], ps_t[q % 2][:, 0:n]), ("onehot copied", q))

        def exponentials(b):
            act.wait("shifted", b)
            act.do(lambda: S.activation(weight[:, b % 2, :, :], shifted[:, :, :], ACT.Exp), ("weights", b))

        def copy_weights(q):
            b, (t0, t1) = q // G, STEP[q % G]
            act.wait("weights", b)
            if q >= 2:
                act.wait("summed", q - 2)
            act.do(lambda: S.copy(wv[:, q % 2, 0:t1 - t0, D:WV],
                                  weight[:, b % 2, :, t0:t1].rearrange("p h t -> p t h")),
                   ("weights beside", q))

        def copy_turned(b):
            act.wait("aggregate turned", b)
            if b >= 1:
                act.wait("times Wo", b - 1)
            act.do(lambda: S.copy(agg_t[:, :], turned(b)), ("turned copied", b))

        def inverse_deviation(b):
            act.wait("moments", b)
            act.do(lambda: S.activation(rstd[:, 0:1], moments[:, 1:2], ACT.Ln, bias=eps_c[:, 0:1]),
                   ("log", b))
            act.wait("log", b)
            act.do(lambda: S.activation(rstd[:, 1:2], rstd[:, 0:1], ACT.Exp, scale=-0.5), ("rstd", b))

        indices(0)
        for q in range(AHEAD):
            build_onehot(q)
        for q in range((NB + 2) * G + 8 + LAG):
            b, g = divmod(q, G)
            old = q - G - LAG
            if q < NB * G:
                turn_onehot(q)
                copy_onehot(q)
            if 1 <= q <= NB * G:
                spread_q(q - 1)
                edge_terms(q - 1)
            maxima = b - 1 if 1 <= b <= NB else None

            def at(part, step):
                if maxima is not None and g == step:
                    part(maxima)

            if g == 7 and b < NB:
                runs_of_dst(b)
            at(exponentials, 4)
            if g == G - AHEAD - 1 and b + 1 < NB:
                indices(b + 1)
            if g == 4 and b < NB:
                dst_of_ends(b)
            if q + AHEAD < NB * G:
                build_onehot(q + AHEAD)
            if 0 <= old < NB * G:
                copy_weights(old)
                weigh(old)
            if q < NB * G:
                multiply(q)
            at(run_maxima, 0)
            at(crossing_maxima, 1)
            at(edge_maxima, 2)
            if g == 4 and b < NB:
                sequence_ends(b)
            if q < NB * G:
                dot(q)
            if 1 <= old <= NB * G:
                sum_step(old - 1)
            at(turn_ends, 1)
            at(turn_crossing, 2)
            if g == 4 and b < NB:
                turn_dst(b)
            for offset, parts in ((1, (divide,)), (2, (turn_aggregate, copy_turned)), (3, (times_wo,)),
                                  (4, (residual,)), (5, (inverse_deviation,)), (7, (normalise,))):
                done, left = divmod(q - 2 * G - LAG - offset, G)
                if 0 <= done < NB and left == 0:
                    for part in parts:
                        part(done)

        for i, w in ((1, Wk), (2, Wv)):
            sp.do(lambda i=i, w=w: nc.sync.dma_start(w_qkv[:, i * D:(i + 1) * D], w).then_inc(s_wkv, 16))
        for k in range(len(s_xt)):
            lo, hi = k * xt_blocks * P, min(N, (k + 1) * xt_blocks * P)
            sp.do(lambda lo=lo, hi=hi, k=k: nc.sync.dma_start(xt[:, lo:hi], x_t[:, lo:hi])
                  .then_inc(s_xt[k], 16))
            if k == 0:
                sp.do(lambda: nc.sync.dma_start(dst2d_i, dst.rearrange("(r c) -> r c", c=RC))
                      .then_inc(s_dst2d, 16))
        sp.do(lambda: nc.sync.dma_start(w_qkv[:, 0:D], Wq).then_inc(s_wrest, 16))
        sp.do(lambda: nc.sync.dma_start(w_o[:, :], Wo).then_inc(s_wrest, 16))
        sp.do(lambda: nc.sync.dma_start(w_e[0:EF, :], We).then_inc(s_wrest, 16))
        sp.do(lambda: nc.sync.dma_start(w_e[EF:EF + 1, :], be.rearrange("(a h) -> a h", a=1))
              .then_inc(s_wrest, 16))
        sp.wait("x zero")
        sp_first = sp.split()

        first = [None]

        def load_indices(b):
            i = b % 2
            if b >= 2:
                sp.wait("product", (b - 1) * G - 1)
                sp.wait("dst", b - 2)

            def read_start():
                first[0] = nc.sync.value_load(start_row[0:1, b:b + 1], min_val=0, max_val=E - C)
            sp.do(read_start)
            for to, frm, s in ((src_i, src, s_src), (dst_i, dst, s_dst)):
                sp.do(lambda to=to, frm=frm, s=s: nc.sync.dma_start(
                    to[:, i, 0:LM], frm[bass.ds(first[0], P * LM)].rearrange("(p l) -> p l", l=LM))
                    .then_inc(s[i], 16))
                for t in range(LM, L):
                    sp.do(lambda to=to, frm=frm, s=s, t=t: nc.sync.dma_start(
                        to[:, i, t:t + 1], frm[bass.ds(first[0] + P * t, P)]
                        .rearrange("(p a) -> p a", a=1)).then_inc(s[i], 16))

        def load_edges(b):
            if b == 0:
                for i in range(STAGES):
                    sp.wait_dma(s_table[i], TABLE_DONE[i])
            if b >= 2:
                sp.wait("edge terms", b - 2)
            sp.do(lambda: nc.sync.dma_start(edge_f[b % 2][0:EF, :], edge_t[:, bass.ds(first[0], C)])
                  .then_inc(s_edge[b % 2], 16))

        def load_x(b):
            if b >= 2:
                sp.wait("residual", b - 2)
            sp.do(lambda: nc.sync.dma_start(x_blk[0:rows(b), b % 2, :], x[b * P:b * P + rows(b), :])
                  .then_inc(s_x[b % 2], 16))

        def store(b):
            sp.wait("normal", b)
            sp.do(lambda: nc.sync.dma_start(out[b * P:b * P + rows(b), :], y_out[0:rows(b), b % 2, :])
                  .then_inc(s_y[b % 2], 16))

        for b in range(NB + 3):
            if b < NB:
                load_indices(b)
                load_edges(b)
            if 2 <= b < NB + 2:
                load_x(b - 2)
            if b >= 3:
                store(b - 3)
        for i in range(2):
            sp.wait_dma(s_y[i], 16 * len(range(i, NB, 2)))

        lines = {}

        def body(name):
            return {n: Line(lines.setdefault(name, {}), sem(f"s_{name}_{n}"))
                    for n in ("sp", "pool", "act", "dve", "pe")}

        chunk, ended = body("chunk"), body("ended")
        s_gfree = sem("s_gfree")
        s_ginit = sem("s_ginit")
        s_gnode = sem("s_gnode")
        s_gload, s_ggather, s_gx, s_gy = (
            sem(n) for n in ("s_gload", "s_ggather", "s_gx", "s_gy"))
        s_gpad = sem("s_gpad")
        s_passed = {n: sem(f"s_passed_{n}") for n in ("sp", "pool", "act", "dve", "pe")}
        x_pad = nc.dram_tensor("x_pad", [NB * P, D], F32).ap()
        y_pad = nc.dram_tensor("y_pad", [NB * P, D], F32).ap()
        now = {}
        GFAR = -1.0e30

        def heads(a, n, inner):
            return a.rearrange("p (h a) -> p h a", a=1).to_broadcast([n, H, inner])

        def chunk_body():
            sp, pool, act, dve, pe = (chunk[n] for n in ("sp", "pool", "act", "dve", "pe"))
            sp.wait_dma(s_gfree, 1)
            for to, frm in ((g_src, src), (g_dst, dst)):
                sp.do(lambda to=to, frm=frm: nc.sync.dma_start(
                    to, frm[bass.ds(now["chunk"] * GP, GP)].rearrange("(p a) -> p a", a=1))
                    .then_inc(s_gload, 16))
            sp.do(lambda: nc.sync.dma_start(g_edge[0:EF, :], edge_t[:, bass.ds(now["chunk"] * GP, GP)])
                  .then_inc(s_gload, 16))
            pool.wait_dma(s_gload, 48)
            pool.do(lambda: nc.gpsimd.indirect_dma_start(
                g_kv, None, kv_table, bass.IndirectOffsetOnAxis(ap=g_src, axis=0)).then_inc(s_ggather, 16))
            dve.wait_dma(s_gload, 48)
            dve.do(lambda: V.tensor_copy(g_dst_f, g_dst), "dst")
            dve.wait("dst")
            dve.do(lambda: V.tensor_scalar(g_hot, iota_n[0:GP, :], g_base[0:GP, :], g_dst_f, ALU.add,
                                           ALU.is_equal), "hot")
            dve.wait("hot")
            dve.do(lambda: V.tensor_reduce(g_in, g_hot, AX.X, ALU.add), "in")
            dve.wait("in")
            dve.do(lambda: V.tensor_scalar(g_far, g_in, -1.0, -GFAR, ALU.add, ALU.mult))
            pe.wait("hot")
            pe.do(lambda: T.transpose(ps_t[0][:, 0:GP], g_hot, ident[0:GP, 0:GP]), "hot turned")
            act.wait("hot turned")
            act.do(lambda: S.copy(g_hot_t, ps_t[0][:, 0:GP]), "hot copied")
            pe.wait("hot copied")
            pe.wait_dma(s_gload, 48)
            pe.do(lambda: T.matmul(ps_q[0][0:GP, 0:D], g_hot_t, q_all[:, bass.ds(now["block"], 1), :]
                                   .rearrange("p a d -> p (a d)"), start=True, stop=True))
            pe.do(lambda: T.matmul(ps_e[0:GP, 0:H], g_edge, w_e[:, :], start=True, stop=True), "q, edge")
            dve.wait("hot copied")
            dve.do(lambda: V.tensor_scalar(g_mask, g_hot_t, -1.0, -FAR, ALU.add, ALU.mult), "mask")
            dve.wait("q, edge")
            dve.wait_dma(s_ggather, 16)
            dve.do(lambda: V.tensor_tensor(g_prod, ps_q[0][0:GP, 0:D], g_kv[:, 0:D], ALU.mult), "prod")
            dve.wait("prod")
            dve.do(lambda: V.tensor_reduce(g_score, g_prod.rearrange("p (h d) -> p h d", d=HD), AX.X,
                                           ALU.add), "dot")
            dve.wait("dot")
            dve.do(lambda: V.tensor_tensor(g_score, g_score, ps_e[0:GP, 0:H], ALU.add), "score")
            dve.wait("score")
            dve.do(lambda: V.tensor_copy(g_spread.rearrange("p (h n) -> p h n", h=H), heads(g_score, GP, P)),
                   "spread")
            pe.wait("spread")
            half = H // 2
            for h in range(H):
                bank = (ps_s, ps_t[1])[h // half]
                pe.do(lambda h=h, bank=bank: T.matmul(
                    bank[:, (h % half) * GP:(h % half + 1) * GP], g_spread[:, h * P:(h + 1) * P],
                    ident[0:GP, 0:GP], start=True, stop=True), "by node" if h == H - 1 else None)
            dve.wait("by node")
            dve.wait("mask")
            z = g_z.rearrange("p (h e) -> p h e", h=H)
            for k, bank in enumerate((ps_s, ps_t[1])):
                dve.do(lambda k=k, bank=bank: V.tensor_tensor(
                    z[:, k * half:(k + 1) * half, :],
                    bank[:, 0:half * GP].rearrange("p (h e) -> p h e", h=half),
                    g_mask.rearrange("p (a e) -> p a e", a=1).to_broadcast([P, half, GP]), ALU.add),
                    "masked" if k else None)
            dve.wait("masked")
            dve.do(lambda: V.tensor_reduce(g_zmax, z, AX.X, ALU.max), "chunk max")
            dve.wait("chunk max")
            dve.do(lambda: V.tensor_tensor(g_new, g_max, g_zmax, ALU.max), "new max")
            dve.wait("new max")
            dve.do(lambda: V.tensor_tensor(g_drop, g_max, g_new, ALU.subtract), "drop")
            act.wait("drop")
            act.do(lambda: S.activation(g_keep, g_drop, ACT.Exp), "keep")
            pe.wait("new max")
            pe.do(lambda: T.matmul(ps_q[1][0:GP, 0:H], g_hot_t, g_new, start=True, stop=True), "max by edge")
            dve.wait("max by edge")
            dve.do(lambda: V.tensor_tensor(g_shift, g_score, ps_q[1][0:GP, 0:H], ALU.subtract), "shift")
            dve.wait("shift")
            dve.do(lambda: V.tensor_scalar(g_shift2, g_shift, g_far, None, ALU.add), "shift far")
            act.wait("shift far")
            act.do(lambda: S.activation(g_wv[:, D:WV], g_shift2, ACT.Exp), "weight")
            dve.wait("weight")
            dve.do(lambda: V.tensor_tensor(
                g_wv[:, 0:D].rearrange("p (h d) -> p h d", d=HD),
                g_kv[:, D:KV].rearrange("p (h d) -> p h d", d=HD), heads(g_wv[:, D:WV], GP, HD), ALU.mult),
                "weighted")
            pe.wait("weighted")
            pe.do(lambda: T.matmul(ps_a[0][:, 0:WV], g_hot, g_wv, start=True, stop=True), "chunk sums")
            dve.do(lambda: V.tensor_copy(g_max, g_new))
            dve.do(lambda: V.tensor_tensor(
                g_acc[:, 0:D].rearrange("p (h d) -> p h d", d=HD),
                g_acc[:, 0:D].rearrange("p (h d) -> p h d", d=HD), heads(g_keep, P, HD), ALU.mult))
            dve.do(lambda: V.tensor_tensor(g_acc[:, D:WV], g_acc[:, D:WV], g_keep, ALU.mult), "rescaled")
            dve.wait("rescaled")
            dve.wait("chunk sums")
            dve.do(lambda: V.tensor_tensor(g_acc, g_acc, ps_a[0][:, 0:WV], ALU.add), "added")
            dve.wait("added")
            dve.do(lambda: V.nop().then_inc(s_gfree, 1))

        def ended_body():
            sp, pool, act, dve, pe = (ended[n] for n in ("sp", "pool", "act", "dve", "pe"))
            sp.wait_dma(s_gnode, 1)
            sp.do(lambda: nc.sync.dma_start(x_blk[:, 0, :], x_pad[bass.ds(now["block"] * P, P), :])
                  .then_inc(s_gx, 16))
            dve.do(lambda: V.tensor_scalar(den[:, :], g_acc[:, D:WV], DEN_EPS, None, ALU.add), "den")
            dve.wait("den")
            dve.do(lambda: V.reciprocal(rec[:, :], den[:, :]), "rec")
            dve.wait("rec")
            dve.do(lambda: V.tensor_tensor(
                agg_n[:, :].rearrange("p (h d) -> p h d", d=HD),
                g_acc[:, 0:D].rearrange("p (h d) -> p h d", d=HD), heads(rec[:, :], P, HD), ALU.mult),
                "aggregate")
            pe.wait("aggregate")
            pe.do(lambda: T.transpose(ps_a[1][:, 0:D], agg_n[:, :], ident[:, :]), "turned")
            act.wait("turned")
            act.do(lambda: S.copy(agg_t[:, :], ps_a[1][:, 0:D]), "turned copied")
            pe.wait("turned copied")
            pe.do(lambda: T.matmul(ps_a[1][:, D:2 * D], agg_t[:, :], w_o[:, :], start=True, stop=True),
                  "times Wo")
            dve.wait("times Wo")
            dve.wait_dma(s_gx, 16)
            dve.do(lambda: V.tensor_tensor(y_sum[:, :], ps_a[1][:, D:2 * D], x_blk[:, 0, :], ALU.add), "res")
            dve.wait("res")
            dve.do(lambda: V.tensor_tensor(y_sum[:, :], y_sum[:, :], bias_bc[:, QKV:QKV + D], ALU.add), "y")
            dve.wait("y")
            dve.do(lambda: V.bn_stats(stats[:, :], y_sum[:, :]), "stats")
            dve.wait("stats")
            dve.do(lambda: V.bn_aggr(moments[:, :], stats[:, :]), "moments")
            act.wait("moments")
            act.do(lambda: S.activation(rstd[:, 0:1], moments[:, 1:2], ACT.Ln, bias=eps_c[:, 0:1]), "log")
            act.wait("log")
            act.do(lambda: S.activation(rstd[:, 1:2], rstd[:, 0:1], ACT.Exp, scale=-0.5), "rstd")
            dve.wait("rstd")
            dve.do(lambda: V.tensor_scalar(y_out[:, 0, :], y_sum[:, :], moments[:, 0:1], rstd[:, 1:2],
                                           ALU.subtract, ALU.mult), "normal")
            sp.wait("normal")
            sp.do(lambda: nc.sync.dma_start(y_pad[bass.ds(now["block"] * P, P), :], y_out[:, 0, :])
                  .then_inc(s_gy, 16))
            sp.wait_dma(s_gy, 16)
            dve.wait("normal")
            dve.do(lambda: V.tensor_scalar(g_base, g_base, float(P), None, ALU.add), "next base")
            dve.wait("next base")
            dve.do(lambda: V.nop().then_inc(s_gnode, 1))

        chunk_body()
        ended_body()

        def general_path(engine, name):
            if name == "dve":
                V.memset(g_base, 0.0)
                V.nop().then_inc(s_gnode, 1)
                V.nop().then_inc(s_gfree, 1)
            if name == "sp":
                engine.dma_start(x_pad[0:N, :], x).then_inc(s_gpad, 16)
                if LAST < P:
                    engine.dma_start(x_pad[N:NB * P, :], x_blk[0:P - LAST, 0, :]).then_inc(s_gpad, 16)
                engine.wait_ge(s_gpad, 16 if LAST == P else 32)
            round_ = engine.alloc_register(f"round_{name}")
            engine.reg_mov(round_, 0)
            with engine.Fori(0, NB) as b:
                lo = engine.value_load(lo_row[0:1, bass.ds(b, 1)], min_val=0, max_val=NCH - 1)
                hi = engine.value_load(hi_row[0:1, bass.ds(b + 1, 1)], min_val=1, max_val=NCH)
                if name == "dve":
                    V.memset(g_max, GFAR)
                    V.memset(g_acc, 0.0).then_inc(s_ginit, 1)
                    engine.wait_ge(s_ginit, b + 1)
                    engine.sem_inc(s_passed[name])
                with engine.Fori(lo, hi) as c:
                    now.update(block=b, chunk=c)
                    chunk[name].emit(engine, engine.snap(round_, min_val=0, max_val=NB * NCH),
                                      s_passed[name])
                    engine.reg_add(round_, round_, 1)
                now.update(block=b)
                ended[name].emit(engine, b, s_passed[name])
            if name == "sp":
                engine.dma_start(out, y_pad[0:N, :]).then_inc(s_y[0], 16)
                engine.wait_ge(s_y[0], 16)

        block = ctx.enter_context(nc.Block())

        def program(engine, name, prologue, fast):
            prologue.emit(engine)
            engine.wait_ge(marks["general",][0].semaphore, marks["general",][1])
            general = engine.value_load(general_i[0:1, 0:1], min_val=0, max_val=2 * E)
            with engine.If(general == 0):
                fast.emit(engine)
            with engine.Else():
                general_path(engine, name)

        @block.sync
        def _(engine):
            program(engine, "sp", sp_first, sp)

        @block.gpsimd
        def _(engine):
            program(engine, "pool", pool_first, pool)

        @block.scalar
        def _(engine):
            program(engine, "act", act_first, act)

        @block.vector
        def _(engine):
            program(engine, "dve", dve_first, dve)

        @block.tensor
        def _(engine):
            program(engine, "pe", pe_first, pe)


_INS = ["x", "src", "dst", "L0_gnn_Wq", "L0_gnn_bq", "L0_gnn_Wk", "L0_gnn_bk", "L0_gnn_Wv", "L0_gnn_bv",
        "L0_gnn_We", "L0_gnn_be", "L0_gnn_Wo", "L0_gnn_bo"]


def kernel(**inputs):
    import numpy as _np
    import concourse.bacc as _bacc
    from concourse import mybir as _mybir
    from concourse.bass_utils import run_bass_kernel_spmd as _run

    nc = _bacc.Bacc("TRN2", target_bir_lowering=False, num_devices=1)
    host = {name: _np.ascontiguousarray(inputs[name]) for name in _INS}
    host["x_t"] = _np.ascontiguousarray(_np.asarray(inputs["x"]).T)
    host["edge_t"] = _np.ascontiguousarray(_np.asarray(inputs["edge_attr_64"]).T)
    arrays, args = {}, {}
    for name, a in host.items():
        arrays[f"in_{name}"] = a
        args[name.replace("L0_gnn_", "")] = nc.dram_tensor(
            f"in_{name}", a.shape, _mybir.dt.from_np(a.dtype), kind="ExternalInput").ap()
    out = nc.dram_tensor("out_0", host["x"].shape, _mybir.dt.float32, kind="ExternalOutput").ap()
    graph_attention(nc, out=out, **args)
    r = _run(nc, [arrays], core_ids=[0])
    return r.results[0]["out_0"]
```
